# Optimizing a Trainium2 kernel written in Bass

```python
import numpy as np
import jax
import jax.numpy as jnp

def _softmax(x, axis=-1):
    return jax.nn.softmax(x, axis=axis)

def _gelu(x):
    return jax.nn.gelu(x, approximate=True)

def _silu(x):
    return jax.nn.silu(x)

def _sigmoid(x):
    return jax.nn.sigmoid(x)

def _layernorm(x, axis=-1, eps=1e-05):
    m = jnp.mean(x, axis=axis, keepdims=True)
    v = jnp.var(x, axis=axis, keepdims=True)
    return (x - m) / jnp.sqrt(v + eps)

def _scatter_add(tgt, idx, src, axis=0):
    return tgt.at[idx].add(src)

def _segment_sum(src, seg, n):
    return jax.ops.segment_sum(src, seg, n)
kernel_name = 'mk_flamingo_gated_d1_seqx_r4_959515'

def setup_inputs(seed: int=0):
    np.random.seed(seed)
    _w = jnp.asarray

    def _rec_inputs():
        import jax
        import jax.numpy as jnp
        _rk = jax.random.key(seed)
        x = 7.22e-05 + 1 * jax.random.normal(jax.random.fold_in(_rk, 1), (4, 512, 512), jnp.float32)
        _lenS = 512 - jax.random.randint(jax.random.fold_in(_rk, 7), (4,), 0, max(1, 512 // 4) + 1, jnp.int32)
        _lenS2 = 512 - jax.random.randint(jax.random.fold_in(_rk, 8), (4,), 0, max(1, 512 // 4) + 1, jnp.int32)
        _ctx_1024P = jax.random.normal(jax.random.fold_in(_rk, 11), (4, 16, 256), jnp.float32)
        _ctx_1024c = jax.random.dirichlet(jax.random.fold_in(_rk, 511), 0.3 * jnp.ones((16,), jnp.float32), (4, 512))
        _ctx_1024t = jnp.einsum('bsk,bkd->bsd', _ctx_1024c, _ctx_1024P)
        _ctx_1024t = _ctx_1024t * jax.lax.rsqrt(jnp.mean(jnp.square(_ctx_1024t)) + 1e-12) * 0.953939
        ctx_1024 = 2.81802e-05 + 1.00001 * (_ctx_1024t + 0.3 * jax.random.normal(jax.random.fold_in(_rk, 611), (4, 512, 256), jnp.float32))
        _g = jax.random.normal(jax.random.fold_in(_rk, 9001), (2, 1), jnp.float32)
        _g = jnp.sign(_g) * jnp.maximum(jnp.abs(_g), 1.0) + (_g == 0) * 1.0
        g_xattn = _g[0]
        g_ffn = _g[1]
        return (x, ctx_1024, g_xattn, g_ffn)
    x, ctx_1024, g_xattn, g_ffn = _rec_inputs()

    def _L0_xattn_setup():
        import jax, jax.numpy as jnp
        import numpy as np
        key = jax.random.key(seed)
        ks = jax.random.split(key, 6)
        B, L, N, C, D = (8, 128, 512, 256, 128)
        return {'teacher_logits': jax.random.normal(ks[0], (B, L, N), dtype=jnp.float32), 'teacher_features': jax.random.normal(ks[1], (B, N, C), dtype=jnp.float32), 'Wq': jax.random.normal(ks[2], (D, C), dtype=jnp.float32) * (1.0 / np.sqrt(C)), 'bq': jnp.zeros((D,), dtype=jnp.float32), 'Wk': jax.random.normal(ks[3], (D, C), dtype=jnp.float32) * (1.0 / np.sqrt(C)), 'bk': jnp.zeros((D,), dtype=jnp.float32)}
    _L0_xattn_all = _L0_xattn_setup()
    _L0_xattn_in = {k: v for k, v in _L0_xattn_all.items() if k in ('Wq', 'bq', 'Wk', 'bk')}
    del _L0_xattn_all

    def _L0_ffn_setup():
        import jax, jax.numpy as jnp
        import numpy as np
        B, S, H, I, E, NS, TOPK = (2, 256, 512, 352, 8, 1, 2)
        SCALE = 1.0
        key = jax.random.key(seed)
        ks = jax.random.split(key, 8)
        init = lambda k, shp: jax.random.normal(k, shp, dtype=jnp.float32) * 0.02
        return dict(x=jax.random.normal(ks[0], (B, S, H), dtype=jnp.float32), router_w=init(ks[1], (E, H)), shared_gate=init(ks[2], (I, H)), shared_up=init(ks[3], (I, H)), shared_down=init(ks[4], (H, I)), w_gate=init(ks[5], (E, I, H)), w_up=init(ks[6], (E, I, H)), w_down=init(ks[7], (E, H, I)))
    _L0_ffn_all = _L0_ffn_setup()
    _L0_ffn_in = {k: v for k, v in _L0_ffn_all.items() if k in ('router_w', 'shared_gate', 'shared_up', 'shared_down', 'w_gate', 'w_up', 'w_down')}
    del _L0_ffn_all
    return {'x': x, 'ctx_1024': ctx_1024, 'g_xattn': g_xattn, 'g_ffn': g_ffn, 'L0_xattn_Wq': _L0_xattn_in['Wq'], 'L0_xattn_bq': _L0_xattn_in['bq'], 'L0_xattn_Wk': _L0_xattn_in['Wk'], 'L0_xattn_bk': _L0_xattn_in['bk'], 'L0_ffn_router_w': _L0_ffn_in['router_w'], 'L0_ffn_shared_gate': _L0_ffn_in['shared_gate'], 'L0_ffn_shared_up': _L0_ffn_in['shared_up'], 'L0_ffn_shared_down': _L0_ffn_in['shared_down'], 'L0_ffn_w_gate': _L0_ffn_in['w_gate'], 'L0_ffn_w_up': _L0_ffn_in['w_up'], 'L0_ffn_w_down': _L0_ffn_in['w_down']}

def reference(x, ctx_1024, g_xattn, g_ffn, L0_xattn_Wq, L0_xattn_bq, L0_xattn_Wk, L0_xattn_bk, L0_ffn_router_w, L0_ffn_shared_gate, L0_ffn_shared_up, L0_ffn_shared_down, L0_ffn_w_gate, L0_ffn_w_up, L0_ffn_w_down):
    import jax
    import jax.numpy as jnp

    def _L0_xattn_ref(teacher_logits, teacher_features, Wq, bq, Wk, bk):
        import jax, jax.numpy as jnp
        import numpy as np
        query = jnp.einsum('bnc,dc->bnd', teacher_features, Wq) + bq
        key = jnp.einsum('bnc,dc->bnd', teacher_features, Wk) + bk
        energy = jnp.einsum('bnd,bmd->bnm', query, key)
        attention = jax.nn.softmax(energy, axis=-1)
        x_m = jnp.einsum('bln,bmn->blm', teacher_logits, attention)
        return x_m

    def _L0_ffn_ref(x, router_w, shared_gate, shared_up, shared_down, w_gate, w_up, w_down):
        import jax, jax.numpy as jnp
        import numpy as np
        B, S, H, I, E, NS, TOPK = (2, 256, 512, 352, 8, 1, 2)
        SCALE = 1.0
        Bs, Ss, Hs = x.shape
        flat = x.reshape(-1, Hs)
        N = flat.shape[0]
        g = flat @ shared_gate.T
        u = flat @ shared_up.T
        shared_out = jax.nn.sigmoid(g) * u @ shared_down.T
        logits = flat @ router_w.T
        weights = jax.nn.softmax(logits, axis=-1)
        top_w, top_idx = jax.lax.top_k(weights, TOPK)
        top_w = top_w * SCALE
        comb = jnp.zeros_like(weights).at[jnp.arange(N)[:, None], top_idx].add(top_w)
        xb = flat.astype(jnp.bfloat16)
        wg = w_gate.astype(jnp.bfloat16)
        wu = w_up.astype(jnp.bfloat16)
        wd = w_down.astype(jnp.bfloat16)
        ge = jnp.einsum('nh,eih->nei', xb, wg)
        ue = jnp.einsum('nh,eih->nei', xb, wu)
        he = jax.nn.sigmoid(ge) * ue
        de = jnp.einsum('nei,ehi->neh', he, wd)
        routed = (comb.astype(jnp.bfloat16)[:, :, None] * de).astype(jnp.float32).sum(axis=1)
        return x + shared_out.reshape(Bs, Ss, Hs) + routed.reshape(Bs, Ss, Hs)
    x = x + jnp.tanh(g_xattn[0]) * _L0_xattn_ref(_layernorm(x, axis=-1), ctx_1024, L0_xattn_Wq, L0_xattn_bq, L0_xattn_Wk, L0_xattn_bk)
    x = x + jnp.tanh(g_ffn[0]) * _L0_ffn_ref(_layernorm(x, axis=-1), L0_ffn_router_w, L0_ffn_shared_gate, L0_ffn_shared_up, L0_ffn_shared_down, L0_ffn_w_gate, L0_ffn_w_up, L0_ffn_w_down)
    return x

_drawn_inputs = setup_inputs


def setup_inputs(seed=0):
    import zlib

    import numpy as np

    out = dict(_drawn_inputs(seed))
    spreads = {'L0_xattn_bq': (0.0, 0.1), 'L0_xattn_bk': (0.0, 0.8)}
    factors = {'L0_ffn_w_gate': 3.101}
    for name, (base, spread) in spreads.items():
        noise = np.random.default_rng([zlib.crc32(name.encode()), seed]).standard_normal(out[name].shape)
        drawn = base * np.exp(spread * noise) if base else spread * noise
        out[name] = jnp.asarray(drawn.astype(out[name].dtype))
    for name, factor in factors.items():
        out[name] = (out[name] * factor).astype(out[name].dtype)
    return out
```

```python
from contextlib import ExitStack

import concourse.bass as bass
from concourse import mybir

ALU = mybir.AluOpType
ACT = mybir.ActivationFunctionType
AX = mybir.AxisListType
F32 = mybir.dt.float32
BF16 = mybir.dt.bfloat16

P = 128
EPS = 1e-5


def gated_block(nc, x, ctxT, g2, wqT, wkT, bq, bk, rwT, sguT, sdT, wguT, wdT, out):
    NB, L, N = x.shape
    C = ctxT.shape[1]
    D = wqT.shape[1]
    E = rwT.shape[1]
    I = sdT.shape[0]
    LT, NT, CT = L // P, N // P, C // P
    KI = [P, P, I - 2 * P]
    IT = len(KI)
    TT = NB * LT
    U = E * TT
    UB = TT // 2

    with ExitStack() as ctx:
        def sb(name, shape, dt=F32):
            return ctx.enter_context(nc.sbuf_tensor(name, shape, dt))

        def sem(name):
            return ctx.enter_context(nc.semaphore(name))

        bank = [ctx.enter_context(nc.psum_tensor(f"bank{i}", [P, 512], F32)) for i in range(8)]
        bankT = [bank[4 + i][:, :].bitcast(BF16) for i in range(2)]

        wq_sb = sb("wq_sb", [P, CT, D])
        wk_sb = sb("wk_sb", [P, CT, D])
        bq_sb = sb("bq_sb", [P, 1])
        bk_sb = sb("bk_sb", [P, 1])
        rw_sb = sb("rw_sb", [P, NT, E])
        sgu_sb = sb("sgu_sb", [P, NT, 2 * I])
        sd_sb = sb("sd_sb", [P, IT, N])
        wgu_sb = sb("wgu_sb", [P, NT, E, 2 * I], BF16)
        g_sb = sb("g_sb", [P, 2])
        tg = sb("tg", [P, 2])
        ones = sb("ones", [P, P])
        ident = sb("ident", [P, P])
        identb = sb("identb", [P, P], BF16)
        half = sb("half", [P, LT])
        inp = sb("inp", [P, 2 * (LT * N + CT * L)])
        xs = inp[:, 0:2 * LT * N].rearrange("p (h j n) -> p h j n", h=2, j=LT)
        cx = inp[:, 2 * LT * N:].rearrange("p (h k l) -> p h k l", h=2, k=CT)
        wd_sb = inp[:, :].bitcast(BF16)[:, 0:IT * E * N].rearrange("p (k e n) -> p k e n", k=IT, e=E)
        st1 = sb("st1", [P, LT, 6])
        mv1 = sb("mv1", [P, LT, 2])
        ve1 = sb("ve1", [P, LT])
        rs1 = sb("rs1", [P, LT])
        lnr = sb("lnr", [P, LT, N])
        turned = sb("turned", [P, 2 * NT * L])
        ln1T = turned[:, 0:NT * L].rearrange("p (k l) -> p k l", k=NT)
        probT = turned[:, NT * L:].rearrange("p (k l) -> p k l", k=NT)
        lnTb = turned[:, :].bitcast(BF16).rearrange("p (k t) -> p k t", k=NT)
        qT = sb("qT", [P, L])
        kT = sb("kT", [P, L])
        nmx = sb("nmx", [P, LT])
        den = sb("den", [P, LT])
        rden = sb("rden", [P, LT])
        prob = sb("prob", [P, LT, L])
        acc = sb("acc", [P, TT, N])
        lnT = sb("lnT", [P, NT, TT * P])
        lnTs = sb("lnTs", [P, NT, P])
        logits = sb("logits", [P, TT, E])
        comb = sb("comb", [P, TT, E])
        rt = [sb(f"rt{i}", [P, TT, E]) for i in range(4)]
        rv = [sb(f"rv{i}", [P, TT]) for i in range(4)]
        sig = lnr[:, 0:2, :]
        hT = prob
        hrow = sb("hrow", [P, 2, I], BF16)
        hTb = sb("hTb", [P, 2, IT, P], BF16)

        s = {n: sem(n) for n in (
            "xin0 xin1 cin0 cin1 wsmall wshared wexp outd "
            "const tgd stat1 eps1 rstd1 ln1 t1 e1 proj qk eng mxd expd rec prb tp ep xmm x1d "
            "stat2 eps2 rstd2 ln2 accd t2 e2 e2s lgm lgd bcast dchain rexp rmax combd gum sigd hd dm acc2 "
            "cgu csig ch ct cev cy cacc").split()}

        block = ctx.enter_context(nc.Block())

        XB = [s["xin0"], s["xin1"]]
        CB = [s["cin0"], s["cin1"]]

        @block.sync
        def _(sp):
            sp.dma_start(wq_sb[:], wqT.rearrange("(k p) d -> p k d", p=P)).then_inc(s["wsmall"], 16)
            sp.dma_start(wk_sb[:], wkT.rearrange("(k p) d -> p k d", p=P)).then_inc(s["wsmall"], 16)
            sp.dma_start(bq_sb[:], bq.rearrange("(d a) -> d a", a=1)).then_inc(s["wsmall"], 16)
            sp.dma_start(bk_sb[:], bk.rearrange("(d a) -> d a", a=1)).then_inc(s["wsmall"], 16)
            sp.dma_start(rw_sb[:], rwT.rearrange("(k p) e -> p k e", p=P)).then_inc(s["wsmall"], 16)
            for j in range(2):
                sp.dma_start(g_sb[:, j:j + 1], g2[j:j + 1, :].to_broadcast([P, 1])).then_inc(s["wsmall"], 16)

            def load(b, half_):
                sp.dma_start(xs[:, half_], x[b].rearrange("(j p) n -> p j n", p=P)).then_inc(XB[half_], 16)
                sp.dma_start(cx[:, half_], ctxT[b].rearrange("(k p) l -> p k l", p=P)).then_inc(CB[half_], 16)
            load(0, 0)
            load(1, 1)
            sp.dma_start(sgu_sb[:], sguT.rearrange("(k p) i -> p k i", p=P)).then_inc(s["wshared"], 16)
            for k in range(IT):
                sp.dma_start(sd_sb[0:KI[k], k, :], sdT[k * P:k * P + KI[k], :]).then_inc(s["wshared"], 16)
            for b in range(2, NB):
                sp.wait_ge(s["x1d"], LT * (b - 1))
                sp.wait_ge(s["proj"], 2 * (b - 1))
                load(b, b % 2)
            for t in range(TT):
                sp.wait_ge(s["cacc"], (E - 1) * TT + t + 1)
                sp.dma_start(out[t * P:(t + 1) * P, :], acc[:, t, :]).then_inc(s["outd"], 16)
            sp.wait_ge(s["outd"], 16 * TT)

        @block.gpsimd
        def _(pool):
            nc.gpsimd.memset(ones[:], 1.0).then_inc(s["const"], 1)
            nc.gpsimd.memset(half[:], -0.5).then_inc(s["const"], 1)
            pool.wait_ge(s["const"], 2)
            nc.gpsimd.affine_select(out=ident[:], in_=ones[:], compare_op=ALU.is_equal, fill=0.0, base=0,
                                    pattern=[[-1, P]], channel_multiplier=1).then_inc(s["const"], 1)
            pool.wait_ge(s["const"], 3)
            nc.gpsimd.tensor_copy(identb[:], ident[:]).then_inc(s["const"], 1)
            for k in range(NT):
                pool.dma_start(wgu_sb[:, k], wguT[:, k * P:(k + 1) * P, :].rearrange("e p i -> p e i")).then_inc(s["wexp"], 16)
            for b in range(NB):
                for n, (eps, rstd) in enumerate((("eps1", "rstd1"), ("eps2", "rstd2"))):
                    pool.wait_ge(s[eps], b + 1)
                    nc.gpsimd.tensor_tensor(rs1[:], ve1[:], half[:], ALU.pow).then_inc(s[rstd], 1)
            pool.wait_ge(s["x1d"], TT)
            for k in range(IT):
                pool.dma_start(wd_sb[0:KI[k], k], wdT[:, k * P:k * P + KI[k], :].rearrange("e p n -> p e n")).then_inc(s["wexp"], 16)
            for b in range(NB):
                pool.wait_ge(s["e2"], LT * (b + 1))
                pool.tensor_copy(lnTb[:, :, b * L:(b + 1) * L], lnT[:, :, b * L:(b + 1) * L]).then_inc(s["bcast"], 1)

        @block.tensor
        def _(pe):
            TB = [bank[4], bank[5]]

            def transposes(src, n):
                for k in range(NT):
                    mm = pe.transpose(TB[n % 2][:, k * P:(k + 1) * P], src[:, k * P:(k + 1) * P], ident[:])
                return mm

            pe.wait_ge(s["const"], 4)
            pe.wait_ge(s["wsmall"], 16 * 7)
            for b in range(NB):
                h = b % 2
                pe.wait_ge(CB[h], 16 * (b // 2 + 1))
                if b:
                    pe.wait_ge(s["expd"], LT * b)
                for n, w in enumerate((wq_sb, wk_sb)):
                    for k in range(CT):
                        mm = pe.matmul(bank[n][:, :], w[:, k, :], cx[:, h, k, :], start=(k == 0), stop=(k == CT - 1))
                    mm.then_inc(s["proj"], 1)
                for j in range(LT):
                    pe.wait_ge(s["ln1"], LT * b + j + 1)
                    if j >= 2:
                        pe.wait_ge(s["e1"], LT * b + j - 1)
                    elif b:
                        pe.wait_ge(s["e2s"], LT * b - 1 + j)
                    transposes(lnr[:, j], j).then_inc(s["t1"], 1)
                pe.wait_ge(s["qk"], 2 * (b + 1))
                for j in range(LT):
                    n = (2, 0, 1)[j % 3]
                    if j == 3:
                        pe.wait_ge(s["expd"], LT * b + 1)
                    pe.matmul(bank[n][:, :], qT[:, j * P:(j + 1) * P], kT[:, :], start=True, stop=True).then_inc(s["eng"], 1)
                for j in range(LT):
                    pe.wait_ge(s["prb"], LT * b + j + 1)
                    if j < 2:
                        pe.wait_ge(s["e1"], LT * b + j + 3)
                    else:
                        pe.wait_ge(s["ep"], LT * b + j - 1)
                    transposes(prob[:, j], j).then_inc(s["tp"], 1)
                pe.wait_ge(s["ep"], LT * (b + 1))
                pe.wait_ge(s["e1"], LT * (b + 1))
                for j in range(LT):
                    if LT * b + j >= 2:
                        pe.wait_ge(s["x1d"], LT * b + j - 1)
                    for k in range(NT):
                        mm = pe.matmul(bank[6 + j % 2][:, :], ln1T[:, k, j * P:(j + 1) * P], probT[:, k, :],
                                       start=(k == 0), stop=(k == NT - 1))
                    mm.then_inc(s["xmm"], 1)
                if b:
                    pe.wait_ge(s["lgd"], b)
                for j in range(LT):
                    pe.wait_ge(s["ln2"], LT * b + j + 1)
                    pe.wait_ge(s["e2s"], LT * b + j - 1) if j >= 2 else pe.wait_ge(s["ep"], LT * b + j + 3)
                    transposes(lnr[:, j], j).then_inc(s["t2"], 1)
                    pe.wait_ge(s["e2s"], LT * b + j + 1)
                    for k in range(NT):
                        mm = pe.matmul(bank[3][:, j * E:(j + 1) * E], lnTs[:, k, :], rw_sb[:, k, :],
                                       start=(k == 0), stop=(k == NT - 1))
                    mm.then_inc(s["lgm"], 1)
            pe.wait_ge(s["wshared"], 16 * (1 + IT))
            pe.wait_ge(s["lgd"], NB)
            pe.wait_ge(s["e2s"], TT)
            pe.wait_ge(s["x1d"], TT)
            pe.wait_ge(s["expd"], TT)
            for b in range(NB):
                pe.wait_ge(s["e2"], LT * (b + 1))
                for c in range(IT):
                    n = IT * b + c
                    if n >= 2:
                        pe.wait_ge(s["hd"], n - 1)
                    for half_ in range(2):
                        for k in range(NT):
                            mm = pe.matmul(bank[2 * (n % 2) + half_][0:KI[c], :],
                                           sgu_sb[:, k, half_ * I + c * P:half_ * I + c * P + KI[c]],
                                           lnT[:, k, b * L:(b + 1) * L], start=(k == 0), stop=(k == NT - 1))
                    mm.then_inc(s["gum"], 1)
                for j in range(LT):
                    pe.wait_ge(s["acc2"], LT * (b - 1) + j + 1) if b else None
                    for k in range(IT - 1):
                        pe.wait_ge(s["hd"], IT * b + k + 1)
                        pe.matmul(bank[4 + j][:, :], hT[:, k, j * P:(j + 1) * P], sd_sb[:, k, :], start=(k == 0), stop=False)
                pe.wait_ge(s["hd"], IT * (b + 1))
                k = IT - 1
                for j in range(LT):
                    pe.matmul(bank[4 + j][:, :], hT[0:KI[k], k, j * P:(j + 1) * P], sd_sb[0:KI[k], k, :],
                              start=False, stop=True).then_inc(s["dm"], 1)
            pe.wait_ge(s["wexp"], 16 * (NT + IT))
            pe.wait_ge(s["bcast"], NB)
            pe.wait_ge(s["acc2"], TT)
            pe.wait_ge(s["hd"], IT * NB)

            def gate_up(e, t, u, q):
                if q is not None:
                    pe.wait_ge(s["ch"], q)
                for half_ in range(2):
                    for k in range(NT):
                        mm = pe.matmul(bank[2 * u + half_][:, 0:I], lnTb[:, k, bass.ds(t * P, P)],
                                       wgu_sb[:, k, e, half_ * I:half_ * I + I],
                                       start=(k == 0), stop=(k == NT - 1))
                mm.then_inc(s["cgu"], 1)

            def turn(u, n, q):
                pe.wait_ge(s["ch"], n)
                if q is not None:
                    pe.wait_ge(s["cev"], q)
                for k in range(IT):
                    mm = pe.transpose(bankT[u][0:KI[k], k * P:(k + 1) * P], hrow[:, u, k * P:k * P + KI[k]], identb[:])
                mm.then_inc(s["ct"], 1)

            def down(e, u, n, q):
                pe.wait_ge(s["cev"], n)
                if q is not None:
                    pe.wait_ge(s["cacc"], q)
                for k in range(IT):
                    mm = pe.matmul(bank[6 + u][:, :], hTb[0:KI[k], u, k, :], wd_sb[0:KI[k], k, e, :],
                                   start=(k == 0), stop=(k == IT - 1))
                mm.then_inc(s["cy"], 1)

            gate_up(0, 0, 0, None)
            gate_up(0, 1, 1, None)
            turn(0, 1, None)
            with pe.Fori(1, U // 2) as i:
                e = i // UB
                ep = (i - 1) // UB
                t = (i % UB) * 2
                gate_up(e, t, 0, 2 * i - 1)
                turn(1, 2 * i, 2 * i - 2)
                down(ep, 0, 2 * i - 1, 2 * i - 2)
                gate_up(e, t + 1, 1, 2 * i)
                turn(0, 2 * i + 1, 2 * i - 1)
                down(ep, 1, 2 * i, 2 * i - 1)
            turn(1, U, U - 2)
            down(E - 1, 0, U - 1, U - 2)
            down(E - 1, 1, U, U - 1)

        @block.scalar
        def _(act):
            act.wait_ge(s["wsmall"], 16 * 7)
            nc.scalar.activation(tg[:], g_sb[:], ACT.Tanh).then_inc(s["tgd"], 1)
            for b in range(NB):
                for n, (dst, bias) in enumerate(((qT, bq_sb), (kT, bk_sb))):
                    act.wait_ge(s["proj"], 2 * b + n + 1)
                    if b and n == 0:
                        act.wait_ge(s["eng"], LT * b)
                    nc.scalar.activation(dst[:], bank[n][:, :], ACT.Identity, bias=bias[:]).then_inc(s["qk"], 1)
                for j in range(LT):
                    act.wait_ge(s["t1"], LT * b + j + 1)
                    if b and j == 0:
                        act.wait_ge(s["xmm"], LT * b)
                    nc.scalar.copy(ln1T[:, :, j * P:(j + 1) * P],
                                   bank[4 + j % 2][:, :].rearrange("p (k l) -> p k l", k=NT)).then_inc(s["e1"], 1)
                for j in range(LT):
                    n = (2, 0, 1)[j % 3]
                    act.wait_ge(s["mxd"], LT * b + j + 1)
                    if b and j == 0:
                        act.wait_ge(s["tp"], LT * b)
                    nc.scalar.activation(prob[:, j, :], bank[n][:, :], ACT.Exp, bias=nmx[:, j:j + 1],
                                         accum_out=den[:, j:j + 1]).then_inc(s["expd"], 1)
                for j in range(LT):
                    act.wait_ge(s["tp"], LT * b + j + 1)
                    nc.scalar.copy(probT[:, :, j * P:(j + 1) * P],
                                   bank[4 + j % 2][:, :].rearrange("p (k l) -> p k l", k=NT)).then_inc(s["ep"], 1)
                for j in range(LT):
                    act.wait_ge(s["t2"], LT * b + j + 1)
                    src = bank[4 + j % 2][:, :].rearrange("p (k l) -> p k l", k=NT)
                    nc.scalar.copy(lnT[:, :, (b * LT + j) * P:(b * LT + j + 1) * P], src).then_inc(s["e2"], 1)
                    if LT * b + j:
                        act.wait_ge(s["lgm"], LT * b + j)
                    nc.scalar.copy(lnTs[:], src).then_inc(s["e2s"], 1)
            act.wait_ge(s["rmax"], 1)
            nc.scalar.activation(rt[0][:], logits[:], ACT.Exp).then_inc(s["rexp"], 1)
            for n in range(IT * NB):
                act.wait_ge(s["gum"], n + 1)
                if n >= 2:
                    act.wait_ge(s["hd"], n - 1)
                m = KI[n % IT]
                nc.scalar.activation(sig[0:m, n % 2, :], bank[2 * (n % 2)][0:m, :], ACT.Sigmoid).then_inc(s["sigd"], 1)

            act.wait_ge(s["hd"], IT * NB)

            def sigmoid(u, n, q):
                act.wait_ge(s["cgu"], n)
                if q is not None:
                    act.wait_ge(s["ch"], q)
                nc.scalar.activation(sig[:, u, 0:I], bank[2 * u][:, 0:I], ACT.Sigmoid).then_inc(s["csig"], 1)

            def evac(u, n, q):
                act.wait_ge(s["ct"], n)
                if q is not None:
                    act.wait_ge(s["cy"], q)
                k = IT - 1
                nc.scalar.copy(hTb[:, u, 0:k, :], bankT[u][:, 0:k * P].rearrange("p (k l) -> p k l", k=k))
                nc.scalar.copy(hTb[0:KI[k], u, k, :], bankT[u][0:KI[k], k * P:(k + 1) * P]).then_inc(s["cev"], 1)

            sigmoid(0, 1, None)
            sigmoid(1, 2, None)
            evac(0, 1, None)
            with act.Fori(1, U // 2) as i:
                sigmoid(0, 2 * i + 1, 2 * i - 1)
                evac(1, 2 * i, 2 * i - 2)
                sigmoid(1, 2 * i + 2, 2 * i)
                evac(0, 2 * i + 1, 2 * i - 1)
            evac(1, U, U - 2)

        @block.vector
        def _(dve):
            chain = [0]

            def link(ins):
                chain[0] += 1
                ins.then_inc(s["dchain"], 1)
                dve.wait_ge(s["dchain"], chain[0])

            def norm(rows, which, b, j):
                link(nc.vector.bn_stats(out=st1[:, j, :], in_=rows))
                nc.vector.bn_aggr(out=mv1[:, j, :], in_=st1[:, j, :]).then_inc(s["stat" + which], 1)

            def eps(which, b):
                dve.wait_ge(s["stat" + which], LT * (b + 1))
                nc.vector.tensor_scalar(ve1[:], mv1[:, :, 1], EPS, None, ALU.add).then_inc(s["eps" + which], 1)

            dve.wait_ge(s["tgd"], 1)
            for b in range(NB):
                h = b % 2
                dve.wait_ge(XB[h], 16 * (b // 2 + 1))
                if b:
                    dve.wait_ge(s["t2"], LT * b)
                for j in range(LT):
                    norm(xs[:, h, j, :], "1", b, j)
                eps("1", b)
                dve.wait_ge(s["rstd1"], b + 1)
                for j in range(LT):
                    nc.vector.tensor_scalar(lnr[:, j, :], xs[:, h, j, :], mv1[:, j, 0:1], rs1[:, j:j + 1],
                                            ALU.subtract, ALU.mult).then_inc(s["ln1"], 1)
                for j in range(LT):
                    n = (2, 0, 1)[j % 3]
                    dve.wait_ge(s["eng"], LT * b + j + 1)
                    nc.vector.tensor_reduce(nmx[:, j:j + 1], bank[n][:, :], AX.X, ALU.max, negate=True).then_inc(s["mxd"], 1)
                for j in range(LT):
                    dve.wait_ge(s["expd"], LT * b + j + 1)
                    link(nc.vector.reciprocal(rden[:, j:j + 1], den[:, j:j + 1]))
                    nc.vector.tensor_scalar(prob[:, j, :], prob[:, j, :], rden[:, j:j + 1], None, ALU.mult).then_inc(s["prb"], 1)
                for j in range(LT):
                    t = LT * b + j
                    dve.wait_ge(s["xmm"], t + 1)
                    nc.vector.scalar_tensor_tensor(out=acc[:, t, :], in0=bank[6 + j % 2][:, :], scalar=tg[:, 0:1],
                                                   in1=xs[:, h, j, :], op0=ALU.mult, op1=ALU.add).then_inc(s["x1d"], 1)
                    dve.wait_ge(s["x1d"], t + 1)
                    norm(acc[:, t, :], "2", b, j)
                eps("2", b)
                dve.wait_ge(s["rstd2"], b + 1)
                dve.wait_ge(s["t1"], LT * (b + 1))
                for j in range(LT):
                    t = LT * b + j
                    nc.vector.tensor_scalar(lnr[:, j, :], acc[:, t, :], mv1[:, j, 0:1], rs1[:, j:j + 1],
                                            ALU.subtract, ALU.mult).then_inc(s["ln2"], 1)
                for j in range(LT):
                    t = LT * b + j
                    dve.wait_ge(s["ln2"], t + 1)
                    nc.vector.scalar_tensor_tensor(out=acc[:, t, :], in0=lnr[:, j, :], scalar=tg[:, 1:2],
                                                   in1=acc[:, t, :], op0=ALU.mult, op1=ALU.add).then_inc(s["accd"], 1)
                dve.wait_ge(s["lgm"], LT * (b + 1))
                nc.vector.tensor_copy(logits[:, LT * b:LT * (b + 1), :],
                                      bank[3][:, 0:LT * E].rearrange("p (j e) -> p j e", e=E)).then_inc(s["lgd"], 1)
            dve.wait_ge(s["lgd"], NB)
            link(nc.vector.tensor_reduce(rv[0][:], logits[:], AX.X, ALU.max))

            def wide(v):
                return v[:].rearrange("p (t a) -> p t a", a=1).to_broadcast([P, TT, E])
            nc.vector.tensor_tensor(logits[:], logits[:], wide(rv[0]), ALU.subtract).then_inc(s["rmax"], 1)
            dve.wait_ge(s["rexp"], 1)
            link(nc.vector.tensor_reduce(rv[1][:], rt[0][:], AX.X, ALU.add))
            link(nc.vector.reciprocal(rv[2][:], rv[1][:]))
            link(nc.vector.tensor_tensor(rt[0][:], rt[0][:], wide(rv[2]), ALU.mult))
            for e in range(E):
                ins = nc.vector.memset(rt[3][:, :, e:e + 1], float(E - e))
            link(ins)
            link(nc.vector.tensor_copy(rt[2][:], rt[0][:]))
            for n in range(2):
                link(nc.vector.tensor_reduce(rv[0][:], rt[2][:], AX.X, ALU.max))
                link(nc.vector.tensor_tensor(rt[1][:], rt[2][:], wide(rv[0]), ALU.is_equal))
                link(nc.vector.tensor_tensor(rt[1][:], rt[1][:], rt[3][:], ALU.mult))
                link(nc.vector.tensor_reduce(rv[1][:], rt[1][:], AX.X, ALU.max))
                link(nc.vector.tensor_tensor(rt[1][:], rt[3][:], wide(rv[1]), ALU.is_equal))
                link(nc.vector.scalar_tensor_tensor(out=rt[2][:], in0=rt[1][:], scalar=-2.0, in1=rt[2][:],
                                                    op0=ALU.mult, op1=ALU.add))
            link(nc.vector.tensor_scalar(rt[1][:], rt[2][:], 0.0, None, ALU.is_lt))
            link(nc.vector.tensor_tensor(comb[:], rt[0][:], rt[1][:], ALU.mult))
            link(nc.vector.tensor_scalar(comb[:], comb[:], tg[:, 1:2], None, ALU.mult))
            for b in range(NB):
                for c in range(IT):
                    n = IT * b + c
                    m = KI[c]
                    dve.wait_ge(s["sigd"], n + 1)
                    if b and c == 0:
                        dve.wait_ge(s["dm"], LT * b)
                    nc.vector.tensor_tensor(hT[0:m, c, :], sig[0:m, n % 2, :], bank[2 * (n % 2) + 1][0:m, :],
                                            ALU.mult).then_inc(s["hd"], 1)
                for j in range(LT):
                    t = LT * b + j
                    dve.wait_ge(s["dm"], t + 1)
                    nc.vector.scalar_tensor_tensor(out=acc[:, t, :], in0=bank[4 + j][:, :], scalar=tg[:, 1:2],
                                                   in1=acc[:, t, :], op0=ALU.mult, op1=ALU.add).then_inc(s["acc2"], 1)

            def hidden(u, n, q):
                dve.wait_ge(s["csig"], n)
                if q is not None:
                    dve.wait_ge(s["ct"], q)
                nc.vector.tensor_tensor(hrow[:, u, :], sig[:, u, 0:I], bank[2 * u + 1][:, 0:I], ALU.mult).then_inc(s["ch"], 1)

            def gather(e, t, u, n):
                dve.wait_ge(s["cy"], n)
                nc.vector.scalar_tensor_tensor(out=acc[:, t, :], in0=bank[6 + u][:, :], scalar=comb[:, t, bass.ds(e, 1)],
                                               in1=acc[:, t, :], op0=ALU.mult, op1=ALU.add).then_inc(s["cacc"], 1)

            dve.wait_ge(s["acc2"], TT)
            hidden(0, 1, None)
            hidden(1, 2, None)
            with dve.Fori(1, U // 2) as i:
                ep = (i - 1) // UB
                t = ((i - 1) % UB) * 2
                hidden(0, 2 * i + 1, 2 * i - 1)
                gather(ep, t, 0, 2 * i - 1)
                hidden(1, 2 * i + 2, 2 * i)
                gather(ep, t + 1, 1, 2 * i)
            gather(E - 1, TT - 2, 0, U - 1)
            gather(E - 1, TT - 1, 1, U)


def kernel(x, ctx_1024, g_xattn, g_ffn, L0_xattn_Wq, L0_xattn_bq, L0_xattn_Wk, L0_xattn_bk, L0_ffn_router_w,
           L0_ffn_shared_gate, L0_ffn_shared_up, L0_ffn_shared_down, L0_ffn_w_gate, L0_ffn_w_up, L0_ffn_w_down):
    import numpy as np
    import concourse.bacc as bacc
    from concourse import mybir as mb
    from concourse.bass_utils import run_bass_kernel_spmd

    T = lambda a: np.asarray(a).swapaxes(-1, -2)
    arrays = {
        "x": x, "ctxT": T(ctx_1024), "g2": np.stack([np.asarray(g_xattn), np.asarray(g_ffn)]),
        "wqT": T(L0_xattn_Wq), "wkT": T(L0_xattn_Wk), "bq": L0_xattn_bq, "bk": L0_xattn_bk,
        "rwT": T(L0_ffn_router_w),
        "sguT": np.concatenate([T(L0_ffn_shared_gate), T(L0_ffn_shared_up)], 1), "sdT": T(L0_ffn_shared_down),
        "wguT": np.concatenate([T(L0_ffn_w_gate), T(L0_ffn_w_up)], 2), "wdT": T(L0_ffn_w_down),
    }
    arrays = {n: np.ascontiguousarray(a) for n, a in arrays.items()}
    nc = bacc.Bacc("TRN2", target_bir_lowering=False, num_devices=1)
    args = [nc.dram_tensor(n, a.shape, mb.dt.from_np(a.dtype), kind="ExternalInput").ap() for n, a in arrays.items()]
    shape = np.asarray(x).shape
    o = nc.dram_tensor("out", (shape[0] * shape[1], shape[2]), mb.dt.float32, kind="ExternalOutput").ap()
    gated_block(nc, *args, o)
    r = run_bass_kernel_spmd(nc, [arrays], core_ids=[0])
    return np.asarray(r.results[0]["out"]).reshape(shape)
```

```python
from contextlib import ExitStack

import concourse.bass as bass
from concourse import mybir

ALU = mybir.AluOpType
ACT = mybir.ActivationFunctionType
AX = mybir.AxisListType
F32 = mybir.dt.float32
F32R = mybir.dt.float32r
BF16 = mybir.dt.bfloat16
U32 = mybir.dt.uint32

P = 128
EPS = 1e-5
TOP = 2


def at_least(eng, sem, n):
    if not isinstance(n, int) or n > 0:
        eng.wait_ge(sem, n)


def gated_block(nc, x, xT, ctxT, g2, wqT, wkT, bq, bk, sguT, sdT, wguT, wdT, out):
    NB, L, N = x.shape
    C = ctxT.shape[1]
    D = wqT.shape[1]
    E = wguT.shape[0]
    I = sdT.shape[0]
    LT, NT, CT = L // P, N // P, C // P
    KI = [P, P, I - 2 * P]
    IT = len(KI)
    TT = NB * LT
    TOK = TT * P
    ROW = N // 2 + 2
    DST, WT = N // 2, N // 2 + 1
    GU = 2 * I + E
    REG = P + TOK
    NE = (TOK * TOP + (P - 1) * E) // P
    SLOTS = 4
    ZS = 6
    QN = NE // SLOTS
    NQ = (NE + 2) // SLOTS + 1
    last_b = NB - 1
    ORDER = [IT - 1] + list(range(IT - 1))

    xg = nc.dram_tensor("xg", (E * REG + P, ROW), U32, kind="Internal").ap()
    z = nc.dram_tensor("z", (TOP * TOK + NE * P, N), BF16, kind="Internal").ap()

    with ExitStack() as ctx:
        def sb(name, shape, dt=F32):
            return ctx.enter_context(nc.sbuf_tensor(name, shape, dt))

        def sem(name):
            return ctx.enter_context(nc.semaphore(name))

        bank = [ctx.enter_context(nc.psum_tensor(f"bank{i}", [P, 512], F32)) for i in range(8)]
        bankXT = bank[4][:, :].bitcast(BF16)
        bankHT = bank[5][:, :].bitcast(BF16)

        bq_sb = sb("bq_sb", [P, 1])
        bk_sb = sb("bk_sb", [P, 1])
        g_sb = sb("g_sb", [P, 2])
        tg = sb("tg", [P, 3])
        less_mean = sb("less_mean", [P, 1])
        ones = sb("ones", [P, P])
        ident = sb("ident", [P, P])
        identb = sb("identb", [P, P], BF16)
        tri = sb("tri", [P, P])
        half = sb("half", [P, LT])
        down_idx = sb("down_idx", [P, LT, E])
        reset = sb("reset", [P, E, LT])
        region0 = sb("region0", [P, E])
        part = sb("part", [P, 1])
        unused_at = sb("unused_at", [P, NE])
        fill_at = sb("fill_at", [P, TT])
        tile_no = sb("tile_no", [P, NE])
        st = [sb(f"st{i}", [P, LT, 6]) for i in range(2)]
        mv = [sb(f"mv{i}", [P, LT, 2]) for i in range(2)]
        ve = [sb(f"ve{i}", [P, LT]) for i in range(2)]
        rs = [sb(f"rs{i}", [P, LT]) for i in range(2)]
        grow = sb("grow", [P, LT])
        drop = sb("drop", [P, LT])
        nmx = sb("nmx", [P, LT])
        den = sb("den", [P, LT])
        rden = sb("rden", [P, LT])
        lgT = sb("lgT", [E, L])
        ra = [sb(f"ra{i}", [P, LT, E]) for i in range(3)]
        rexp_sb = sb("rexp_sb", [P, LT, E])
        mask = [sb(f"mask{i}", [P, LT, E]) for i in range(TOP)]
        picked = sb("picked", [P, LT, E])
        rv = [sb(f"rv{i}", [P, LT]) for i in range(3)]
        tot = sb("tot", [P, E, LT])
        upto = sb("upto", [P, E, LT])
        before = sb("before", [P, E, LT])
        filled = sb("filled", [P, E + 1])
        cw = sb("cw", [P, TOP, LT])
        cwg = sb("cwg", [P, TOP, LT])
        slot = sb("slot", [P, TOP, LT], U32)
        carrier = sb("carrier", [P, LT])
        cnt = sb("cnt", [P, E])
        ntile = sb("ntile", [P, E])
        tend = sb("tend", [P, E])
        skip = sb("skip", [P, E])
        ahead = sb("ahead", [P, E])
        big = sb("big", [P, max(NE, TT), E])
        big2 = sb("big2", [P, NE, E])
        etab = sb("etab", [P, SLOTS * (NQ + 1)])
        tf = sb("tf", [P, NE])
        limit = sb("limit", [P, NE])
        epack = [sb(f"epack{i}", [P, NQ]) for i in range(2)]
        epack_i = sb("epack_i", [P, NQ], U32)
        erow = sb("erow", [P, NE], U32)
        padr = sb("padr", [P, ROW], U32)
        again = sb("again", [P, NE], U32)
        over = sb("over", [P, NE])
        dest = sb("dest", [P, NE], U32)
        wt = sb("wt", [P, NE], U32)
        desti = sb("desti", [P, SLOTS], U32)
        lnb = sb("lnb", [P, LT, ROW], U32)
        acc = sb("acc", [P, TT, N])
        KP = NT // 2
        wgu_lo = sb("wgu_lo", [P, KP, E, 2 * I], BF16)

        top = -(-nc.sbuf_base // 32) * 32

        def place(items, start):
            made = []
            for name, shape, dt in items:
                start = -(-start // 32) * 32
                made.append(nc.alloc_sbuf_tensor_at(name, shape, dt, offset=start))
                n = 1
                for d in shape[1:]:
                    n *= d
                start += n * (2 if dt == BF16 else 4)
            assert start <= nc.sbuf_usable_end, (start, nc.sbuf_usable_end)
            return made, start

        (lnT_hi, lnT_lo), lnT_end = place((
            ("lnT_hi", [P, NT, L], F32R), ("lnT_lo", [P, NT, L], F32R)), top)
        (hT_hi, hT_lo), hT_end = place((
            ("hT_hi", [P, IT, L], F32R), ("hT_lo", [P, IT, L], F32R)), lnT_end)
        (sig, sgu_hi, sgu_lo, sd_hi, sd_lo), att = place((
            ("sig", [P, 2, L], F32),
            ("sgu_hi", [P, NT, GU], F32R), ("sgu_lo", [P, NT, GU], F32R),
            ("sd_hi", [P, IT, N], F32R), ("sd_lo", [P, IT, N], F32R)), hT_end)
        (xT_raw, cx, wq_sb, wk_sb, q_hi, q_lo, k_hi, k_lo, prob, xT_hi, xT_lo, probT_hi, probT_lo, lnr2), _end = place((
            ("xT_raw", [P, NT, L], F32), ("cx", [P, CT, L], F32), ("wq_sb", [P, CT, D], F32), ("wk_sb", [P, CT, D], F32),
            ("q_hi", [P, L], F32R), ("q_lo", [P, L], F32R), ("k_hi", [P, L], F32R), ("k_lo", [P, L], F32R),
            ("prob", [P, LT, L], F32), ("xT_hi", [P, NT, L], F32R), ("xT_lo", [P, NT, L], F32R),
            ("probT_hi", [P, NT, L], F32R), ("probT_lo", [P, NT, L], F32R), ("lnr2", [P, LT, N], F32)), att)
        (sgu_raw,), _ = place((("sgu_raw", [P, NT, GU], F32),), top)
        (sd_raw,), _ = place((("sd_raw", [P, IT, N], F32),), lnT_end)
        (xt, xTb, hrow, hTb, sigc, ysb), c_end = place((
            ("xt", [P, SLOTS, ROW], U32), ("xTb", [P, 2, NT, P], BF16), ("hrow", [P, 2, IT * P], BF16),
            ("hTb", [P, 2, IT, P], BF16), ("sigc", [P, 2, I], F32), ("ysb", [P, SLOTS, N], BF16)), top)
        assert c_end <= lnT_end
        (zb,), z_end = place((("zb", [P, ZS, TOP, N], BF16),), lnT_end)
        assert z_end <= hT_end
        (wgu_hi, wd_sb), w_end = place((
            ("wgu_hi", [P, NT - KP, E, 2 * I], BF16), ("wd_sb", [P, IT, E, N], BF16)), att)
        assert w_end <= _end
        xtb = xt[:].rearrange("p s r -> p (s r)").bitcast(BF16).rearrange("p (s r) -> p s r", s=SLOTS)

        def wgu(k, e, lo, n):
            return wgu_lo[:, k, e, lo:lo + n] if k < KP else wgu_hi[:, k - KP, e, lo:lo + n]

        s = {n: sem(n) for n in (
            "ctx_in w_in small_in sgu_in sd_in wgu_in wgu2_in wd_in const gates split_hi split_lo "
            "stat1 var1 rstd1 stat2 var2 rstd2 coef ln2 proj qhi qlo t2 lnThi lnTlo xThi xTlo probT probTlo eng nmax expd rden prb tp "
            "xmm x1 base lgcopy lgT lgshift rexp pick rank place placed scat rowsb sgate sup sigd hid hhi hlo dm shared "
            "xT_in padrows padout tabs cxt xev cgu csig ch ct cev cy yev dchain pchain didx zsum comb outd").split()}
        s_xl = [sem(f"xt_in{i}") for i in range(SLOTS)]
        s_yd = [sem(f"y_out{i}") for i in range(SLOTS)]
        s_zl = [sem(f"z_in{i}") for i in range(ZS)]
        X_IN = [sem(f"x_in{b}") for b in range(NB)]

        CONSTS = 15

        block = ctx.enter_context(nc.Block())

        @block.sync
        def _(sp):
            def load_x(b):
                sp.dma_start(acc[:, LT * b:LT * (b + 1), :], x[b].rearrange("(j p) n -> p j n", p=P)).then_inc(X_IN[b], 16)

            def load_ctx(b):
                sp.dma_start(cx[:], ctxT[b].rearrange("(k p) l -> p k l", p=P)).then_inc(s["ctx_in"], 16)

            def load_xT(b):
                sp.dma_start(xT_raw[:], xT[b].rearrange("(k p) l -> p k l", p=P)).then_inc(s["xT_in"], 16)

            sp.dma_start(wq_sb[:], wqT.rearrange("(k p) d -> p k d", p=P)).then_inc(s["w_in"], 16)
            sp.dma_start(wk_sb[:], wkT.rearrange("(k p) d -> p k d", p=P)).then_inc(s["w_in"], 16)
            load_ctx(0)
            sp.dma_start(bq_sb[:], bq.rearrange("(d a) -> d a", a=1)).then_inc(s["small_in"], 16)
            sp.dma_start(bk_sb[:], bk.rearrange("(d a) -> d a", a=1)).then_inc(s["small_in"], 16)
            for j in range(2):
                sp.dma_start(g_sb[:, j:j + 1], g2[j:j + 1, :].to_broadcast([P, 1])).then_inc(s["small_in"], 16)
            load_xT(0)
            load_x(0)
            sp.dma_start(sgu_raw[:], sguT.rearrange("(k p) i -> p k i", p=P)).then_inc(s["sgu_in"], 16)
            for k in range(IT):
                sp.dma_start(sd_raw[0:KI[k], k, :], sdT[k * P:k * P + KI[k], :]).then_inc(s["sd_in"], 16)
            sp.wait_ge(s["padrows"], 1)
            for e in range(E + 1):
                sp.dma_start(xg[e * REG:e * REG + P, :], padr[:]).then_inc(s["padout"], 16)
            for b in range(1, NB):
                sp.wait_ge(s["proj"], 2 * b)
                load_ctx(b)
                sp.wait_ge(s["xThi"], b)
                sp.wait_ge(s["xTlo"], b)
                load_xT(b)
                load_x(b)
            sp.wait_ge(s["padout"], 16 * (E + 1))
            sp.wait_ge(s["scat"], 16 * TOP * TT)
            sp.wait_ge(s["tabs"], 1)
            sp.wait_ge(s["sup"], IT * NB)

            def load_tile(u, slot_, free):
                if free is not None:
                    sp.wait_ge(s["xev"], free)
                row = sp.value_load(erow[0:1, bass.ds(u, 1)], min_val=0, max_val=E * REG)
                sp.dma_start(xt[:, slot_, :], xg[bass.ds(row, P), :]).then_inc(s_xl[slot_], 16)

            for r in range(SLOTS):
                load_tile(r, r, None)
            with sp.Fori(1, QN) as q:
                for r in range(SLOTS):
                    load_tile(SLOTS * q + r, r, SLOTS * q + r - SLOTS + 1)
            for u in range(SLOTS * QN, NE):
                load_tile(u, u % SLOTS, u - SLOTS + 1)
            sp.wait_ge(s["dm"], TT)
            for r in range(SLOTS):
                sp.wait_ge(s_yd[r], 16 * len(range(r, NE, SLOTS)))
            zt = z[0:TOP * TOK, :].rearrange("(c t p) n -> t p c n", c=TOP, p=P)

            def store(t):
                sp.wait_ge(s["comb"], t + 1)
                sp.dma_start(out[t * P:(t + 1) * P, :], acc[:, t, :]).then_inc(s["outd"], 16)
            for t in range(TT):
                if t >= ZS:
                    store(t - ZS)
                sp.dma_start(zb[:, t % ZS], zt[t]).then_inc(s_zl[t % ZS], 16)
            for t in range(TT - ZS, TT):
                store(t)
            sp.wait_ge(s["outd"], 16 * TT)

        @block.gpsimd
        def _(pool):
            nc.gpsimd.memset(ones[:], 1.0).then_inc(s["const"], 1)
            nc.gpsimd.memset(half[:], -0.5).then_inc(s["const"], 1)
            pool.wait_ge(s["const"], 2)
            nc.gpsimd.affine_select(out=ident[:], in_=ones[:], compare_op=ALU.is_equal, fill=0.0, base=0,
                                    pattern=[[-1, P]], channel_multiplier=1).then_inc(s["const"], 1)
            nc.gpsimd.affine_select(out=tri[:], in_=ones[:], compare_op=ALU.is_gt, fill=0.0, base=0,
                                    pattern=[[1, P]], channel_multiplier=-1).then_inc(s["const"], 1)
            pool.wait_ge(s["const"], 4)
            nc.gpsimd.tensor_copy(identb[:], ident[:]).then_inc(s["const"], 1)

            def iota(t, pattern, base, mult=0):
                nc.gpsimd.iota(t, pattern, base=base, channel_multiplier=mult,
                               allow_small_or_imprecise_dtypes=True).then_inc(s["const"], 1)
            iota(down_idx[:], [[0, LT], [-1, E]], E)
            iota(region0[:], [[REG, E]], P)
            iota(filled[:], [[REG, E + 1]], P)
            nc.gpsimd.memset(less_mean[:], -1.0 / N).then_inc(s["const"], 1)
            iota(part[:], [[0, 1]], 0, 1)
            iota(unused_at[:], [[P, NE]], TOP * TOK, 1)
            iota(fill_at[:], [[P, TT]], 0)
            iota(tile_no[:], [[1, NE]], 0)
            nc.gpsimd.memset(reset[:, :, 1:LT], 1.0).then_inc(s["const"], 1)
            nc.gpsimd.memset(reset[:, :, 0:1], 0.0).then_inc(s["const"], 1)

            nc.gpsimd.memset(padr[:], 0).then_inc(s["padrows"], 1)

            chain = [0]

            def link(ins):
                chain[0] += 1
                ins.then_inc(s["pchain"], 1)
                pool.wait_ge(s["pchain"], chain[0])

            def gate(c):
                return tg[:, c:c + 1].to_broadcast([P, LT])

            def factor1(b):
                pool.wait_ge(s["var1"], b + 1)
                link(nc.gpsimd.tensor_tensor(rs[0][:], ve[0][:], half[:], ALU.pow))
                nc.gpsimd.tensor_tensor(rs[0][:], rs[0][:], gate(0), ALU.mult).then_inc(s["rstd1"], 1)

            def factors2(b):
                pool.wait_ge(s["var2"], b + 1)
                nc.gpsimd.tensor_tensor(rs[1][:], ve[1][:], half[:], ALU.pow).then_inc(s["rstd2"], 1)
                pool.wait_ge(s["rstd2"], b + 1)
                if b:
                    pool.wait_ge(s["base"], LT * b)
                link(nc.gpsimd.tensor_tensor(grow[:], rs[1][:], gate(1), ALU.mult))
                link(nc.gpsimd.tensor_tensor(grow[:], grow[:], ones[:, 0:LT], ALU.add))
                link(nc.gpsimd.tensor_tensor(drop[:], rs[1][:], gate(2), ALU.mult))
                nc.gpsimd.tensor_tensor(drop[:], drop[:], mv[1][:, :, 0], ALU.mult).then_inc(s["coef"], 1)

            def x_low(b):
                pool.wait_ge(s["xThi"], b + 1)
                at_least(pool, s["xmm"], LT * b)
                nc.gpsimd.tensor_tensor(xT_lo[:], xT_raw[:], xT_hi[:].bitcast(F32), ALU.subtract).then_inc(s["xTlo"], 1)

            pool.wait_ge(s["gates"], 2)
            x_low(0)
            factor1(0)
            pool.wait_ge(s["sd_in"], 16 * IT)
            for k in range(KP):
                pool.dma_start(wgu_lo[:, k], wguT[:, k * P:(k + 1) * P, :].rearrange("e p i -> p e i")).then_inc(s["wgu_in"], 16)
            pool.wait_ge(s["split_hi"], 1)
            nc.gpsimd.tensor_tensor(sgu_lo[:], sgu_raw[:], sgu_hi[:].bitcast(F32), ALU.subtract).then_inc(s["split_lo"], 1)
            for k in range(IT):
                pool.wait_ge(s["split_hi"], 2 + k)
                nc.gpsimd.tensor_tensor(sd_lo[0:KI[k], k, :], sd_raw[0:KI[k], k, :], sd_hi[0:KI[k], k, :].bitcast(F32),
                                        ALU.subtract).then_inc(s["split_lo"], 1)

            lnbf = lnb[:].rearrange("p j r -> p (j r)").bitcast(BF16).rearrange("p (j r) -> p j r", j=LT)
            lnbw = lnb[:].bitcast(F32)

            def hidden_low(b, c):
                n = IT * b + c
                m = KI[ORDER[c]]
                pool.wait_ge(s["hhi"], n + 1)
                nc.gpsimd.tensor_tensor(hT_lo[0:m, ORDER[c], :], sig[0:m, n % 2, :], hT_hi[0:m, ORDER[c], :].bitcast(F32),
                                        ALU.subtract).then_inc(s["hlo"], 1)

            def scatter(b, c):
                if c:
                    pool.wait_ge(s["scat"], 16 * LT * (TOP * b + c))
                link(nc.gpsimd.iota(lnb[:, :, DST:DST + 1], [[P, LT], [0, 1]], base=c * TOK + b * L, channel_multiplier=1))
                pool.wait_ge(s["placed"], b + 1)
                link(nc.gpsimd.tensor_copy(lnbw[:, :, WT], cwg[:, c, :]))
                for j in range(LT):
                    nc.gpsimd.indirect_dma_start(
                        out=xg, out_offset=bass.IndirectOffsetOnAxis(ap=slot[:, c, j:j + 1], axis=0),
                        in_=lnb[:, j, :], in_offset=None).then_inc(s["scat"], 16)

            for b in range(NB):
                if b == last_b:
                    pool.wait_ge(s["tp"], TT)
                    pool.wait_ge(s["eng"], TT)
                    for k in range(KP, NT):
                        pool.dma_start(wgu_hi[:, k - KP], wguT[:, k * P:(k + 1) * P, :].rearrange("e p i -> p e i")).then_inc(s["wgu2_in"], 16)
                factors2(b)
                if b == last_b:
                    pool.wait_ge(s["xmm"], TT)
                    for k in range(IT):
                        pool.dma_start(wd_sb[0:KI[k], k], wdT[:, k * P:k * P + KI[k], :].rearrange("e p n -> p e n")).then_inc(s["wd_in"], 16)
                pool.wait_ge(s["ln2"], LT * (b + 1))
                if b:
                    pool.wait_ge(s["scat"], 16 * TOP * LT * b)
                nc.gpsimd.tensor_copy(lnbf[:, :, 0:N], lnr2[:]).then_inc(s["rowsb"], 1)
                pool.wait_ge(s["rowsb"], b + 1)
                if b == 0:
                    pool.wait_ge(s["padout"], 16 * (E + 1))
                if b < last_b:
                    x_low(b + 1)
                    factor1(b + 1)
                hidden_low(b, 0)
                hidden_low(b, 1)
                scatter(b, 0)
                hidden_low(b, 2)
                scatter(b, 1)

            def send(u, r, q):
                pool.wait_ge(s["yev"], u + 1)
                if q is not None:
                    pool.wait_ge(s_yd[r], 16 * q)
                nc.gpsimd.tensor_copy(desti[:, r:r + 1], dest[:, bass.ds(u, 1)]).then_inc(s["didx"], 1)
                pool.wait_ge(s["didx"], u + 1)
                nc.gpsimd.tensor_tensor(carrier[:], half[:], half[:], ALU.add)
                nc.gpsimd.indirect_dma_start(
                    out=z, out_offset=bass.IndirectOffsetOnAxis(ap=desti[:, r:r + 1], axis=0),
                    in_=ysb[:, r, :], in_offset=None).then_inc(s_yd[r], 16)

            for r in range(SLOTS):
                send(r, r, None)
            with pool.Fori(1, QN) as q:
                for r in range(SLOTS):
                    send(SLOTS * q + r, r, q)
            for u in range(SLOTS * QN, NE):
                send(u, u % SLOTS, QN)

        @block.tensor
        def _(pe):
            def turn(src, n):
                for k in range(NT):
                    mm = pe.transpose(bank[4 + n % 2][:, k * P:(k + 1) * P], src[:, k * P:(k + 1) * P], ident[:])
                return mm

            def three(dst, a_hi, a_lo, b_hi, b_lo, first, last_):
                pe.matmul(dst, a_lo, b_hi, start=first, stop=False)
                pe.matmul(dst, a_hi, b_lo, start=False, stop=False)
                return pe.matmul(dst, a_hi, b_hi, start=False, stop=last_)

            def project(b):
                pe.wait_ge(s["ctx_in"], 16 * (b + 1))
                if b == 1:
                    pe.wait_ge(s["expd"], LT)
                elif b > 1:
                    pe.wait_ge(s["hid"], IT * (b - 2) + 2)
                for n, w in enumerate((wq_sb, wk_sb)):
                    for k in range(CT):
                        mm = pe.matmul(bank[n][:, :], w[:, k, :], cx[:, k, :], start=(k == 0), stop=(k == CT - 1))
                    mm.then_inc(s["proj"], 1)

            def energy(b, j):
                if j < 2:
                    pe.wait_ge(s["qlo"], 2 * (b + 1))
                else:
                    pe.wait_ge(s["expd"], LT * b + j - 1)
                tok = slice(j * P, (j + 1) * P)
                three(bank[j % 2][:, :], q_hi[:, tok], q_lo[:, tok], k_hi[:], k_lo[:], True, True).then_inc(s["eng"], 1)

            def turn_prob(b, j):
                pe.wait_ge(s["prb"], LT * b + j + 1)
                if j >= 2:
                    pe.wait_ge(s["probTlo"], LT * b + j - 1)
                elif b:
                    pe.wait_ge(s["lnTlo"], LT * (b - 1) + j + 3)
                turn(prob[:, j], j).then_inc(s["tp"], 1)

            def mix(b):
                pe.wait_ge(s["probTlo"], LT * (b + 1))
                pe.wait_ge(s["xTlo"], b + 1)
                for j in range(LT):
                    if j >= 2:
                        pe.wait_ge(s["x1"], LT * b + j - 1)
                    elif b:
                        pe.wait_ge(s["place"], b)
                    for k in range(NT):
                        mm = three(bank[6 + j % 2][:, :], xT_hi[:, k, j * P:(j + 1) * P], xT_lo[:, k, j * P:(j + 1) * P],
                                   probT_hi[:, k, :], probT_lo[:, k, :], k == 0, k == NT - 1)
                    mm.then_inc(s["xmm"], 1)

            def turn_ln2(b, j):
                pe.wait_ge(s["ln2"], LT * b + j + 1)
                if j >= 2:
                    pe.wait_ge(s["lnTlo"], LT * b + j - 1)
                else:
                    pe.wait_ge(s["probTlo"], LT * b + j + 3)
                turn(lnr2[:, j], j).then_inc(s["t2"], 1)

            def turn_logits(b):
                pe.wait_ge(s["lgcopy"], b + 1)
                if b:
                    pe.wait_ge(s["shared"], LT * b)
                else:
                    pe.wait_ge(s["x1"], LT)
                for j in range(LT):
                    mm = pe.transpose(bank[7][:, j * E:(j + 1) * E], lgT[:, j * P:(j + 1) * P], ident[0:E, 0:E])
                mm.then_inc(s["lgT"], 1)

            def rank(b):
                pe.wait_ge(s["pick"], b + 1)
                sel = picked[:].rearrange("p j e -> p (j e)")
                pe.matmul(bank[6][:, 0:LT * E], tri[:], sel, start=True, stop=True)
                pe.matmul(bank[6][:, LT * E:2 * LT * E], ones[:], sel, start=True, stop=True).then_inc(s["rank"], 1)

            def wide_shared(b, c, half_):
                n = IT * b + c
                row = ORDER[c]
                m = KI[row] + (E if half_ and row == IT - 1 else 0)
                free, done = (("sigd", "sgate"), ("hid", "sup"))[half_]
                pair = 0 if c == 1 else 2
                if n == 0:
                    pe.wait_ge(s["split_lo"], 1)
                pe.wait_ge(s["lnTlo"], LT * (b + 1))
                if c == 0:
                    at_least(pe, s[free], IT * b)
                elif c == 1:
                    pe.wait_ge(s["expd"], min(LT * (b + 2), TT))
                else:
                    pe.wait_ge(s[free], IT * b + 1)
                o_ = half_ * I + row * P
                for k in range(NT):
                    mm = three(bank[pair + half_][0:m, :], sgu_hi[:, k, o_:o_ + m], sgu_lo[:, k, o_:o_ + m],
                               lnT_hi[:, k, :], lnT_lo[:, k, :], k == 0, k == NT - 1)
                mm.then_inc(s[done], 1)

            def down(b):
                if b == 0:
                    pe.wait_ge(s["split_lo"], 1 + IT)
                for j in range(LT):
                    if j >= 2:
                        pe.wait_ge(s["shared"], LT * b + j - 1)
                    elif b < last_b:
                        pe.wait_ge(s["x1"], LT * (b + 1) + j + 3)
                    else:
                        pe.wait_ge(s["place"], b + 1)
                    tok = slice(j * P, (j + 1) * P)
                    for c in range(IT):
                        pe.wait_ge(s["hlo"], IT * b + c + 1)
                        k = ORDER[c]
                        m = KI[k]
                        mm = three(bank[6 + j % 2][:, :], hT_hi[0:m, k, tok], hT_lo[0:m, k, tok],
                                   sd_hi[0:m, k, :], sd_lo[0:m, k, :], c == 0, c == IT - 1)
                    mm.then_inc(s["dm"], 1)

            pe.wait_ge(s["w_in"], 16 * 2)
            project(0)
            for j in range(LT):
                energy(0, j)
            pe.wait_ge(s["const"], CONSTS)
            for j in range(LT):
                turn_prob(0, j)
            for b in range(NB):
                more = b < last_b
                mix(b)
                if more:
                    project(b + 1)
                if b:
                    down(b - 1)
                if more:
                    energy(b + 1, 0)
                turn_ln2(b, 0)
                turn_ln2(b, 1)
                if more:
                    energy(b + 1, 1)
                turn_ln2(b, 2)
                turn_ln2(b, 3)
                if more:
                    energy(b + 1, 2)
                    energy(b + 1, 3)
                wide_shared(b, 0, 1)
                wide_shared(b, 0, 0)
                turn_logits(b)
                wide_shared(b, 1, 0)
                wide_shared(b, 1, 1)
                rank(b)
                if more:
                    turn_prob(b + 1, 0)
                    turn_prob(b + 1, 1)
                wide_shared(b, 2, 0)
                if more:
                    turn_prob(b + 1, 2)
                    turn_prob(b + 1, 3)
                wide_shared(b, 2, 1)
            down(last_b)

            def experts(q):
                w = pe.value_load(epack_i[0:1, bass.ds(q, 1)], min_val=0, max_val=E ** (2 * SLOTS - 1) - 1)
                return [(w // E ** i) % E for i in range(2 * SLOTS - 1)]

            def rows_in(u, r, q):
                pe.wait_ge(s_xl[r], 16 * (q + 1))
                at_least(pe, s["xev"], u)
                for k in range(NT):
                    mm = pe.transpose(bankXT[:, k * P:(k + 1) * P], xtb[:, r, k * P:(k + 1) * P], identb[:])
                mm.then_inc(s["cxt"], 1)

            def wide(u, v, e):
                pe.wait_ge(s["xev"], u + 1)
                at_least(pe, s["ch"], u - 1)
                for half_ in range(2):
                    for k in range(NT):
                        mm = pe.matmul(bank[2 * v + half_][:, 0:I], xTb[:, v, k, :], wgu(k, bass.ds(e, 1), half_ * I, I),
                                       start=(k == 0), stop=(k == NT - 1))
                mm.then_inc(s["cgu"], 1)

            def turn_hidden(u, v):
                pe.wait_ge(s["ch"], u + 1)
                at_least(pe, s["cev"], u)
                for k in range(IT):
                    mm = pe.transpose(bankHT[:, k * P:(k + 1) * P], hrow[:, v, k * P:(k + 1) * P], identb[:])
                mm.then_inc(s["ct"], 1)

            def narrow(u, v, e):
                pe.wait_ge(s["cev"], u + 1)
                at_least(pe, s["yev"], u - 1)
                for k in range(IT):
                    mm = pe.matmul(bank[6 + v][:, :], hTb[0:KI[k], v, k, :], wd_sb[0:KI[k], k, bass.ds(e, 1), :],
                                   start=(k == 0), stop=(k == IT - 1))
                mm.then_inc(s["cy"], 1)

            def step(q, r, ids):
                u = SLOTS * q + r
                known = isinstance(u, int)
                if not known or 2 <= u <= NE + 1:
                    turn_hidden(u - 2, r % 2)
                if not known or u >= 3:
                    narrow(u - 3, (r - 3) % 2, ids[r])
                if not known or u + 1 < NE:
                    rows_in(u + 1, (r + 1) % SLOTS, q + 1 if r == SLOTS - 1 else q)
                if not known or u < NE:
                    wide(u, r % 2, ids[r + SLOTS - 1])

            pe.wait_ge(s["tabs"], 1)
            pe.wait_ge(s["lnTlo"], TT)
            rows_in(0, 0, 0)
            pe.wait_ge(s["hid"], IT * NB)
            pe.wait_ge(s["shared"], TT)
            pe.wait_ge(s["wgu_in"], 16 * KP)
            pe.wait_ge(s["wgu2_in"], 16 * (NT - KP))
            pe.wait_ge(s["wd_in"], 16 * IT)
            for q in range(2):
                ids = experts(q)
                for r in range(SLOTS):
                    step(q, r, ids)
            with pe.Fori(2, QN) as q:
                ids = experts(q)
                for r in range(SLOTS):
                    step(q, r, ids)
            for u in range(SLOTS * QN, NE + 3):
                if u % SLOTS == 0:
                    ids = experts(u // SLOTS)
                step(u // SLOTS, u % SLOTS, ids)

            pe.wait_ge(s["yev"], NE)
            for t in range(TT):
                pe.wait_ge(s_zl[t % ZS], 16 * (t // ZS + 1))
                at_least(pe, s["comb"], t - 3)
                for c in range(TOP):
                    mm = pe.matmul(bank[t % 4][:, :], identb[:], zb[:, t % ZS, c, :], start=(c == 0), stop=(c == TOP - 1))
                mm.then_inc(s["zsum"], 1)

        @block.scalar
        def _(act):
            def leave(dst, n, done):
                act.copy(dst, bank[4 + n % 2][:, :].rearrange("p (k l) -> p k l", k=NT)).then_inc(s[done], 1)

            def qk(b):
                at_least(act, s["eng"], LT * b)
                for n, (dst, bias) in enumerate(((q_hi, bq_sb), (k_hi, bk_sb))):
                    act.wait_ge(s["proj"], 2 * b + n + 1)
                    act.activation(dst[:], bank[n][:, :], ACT.Identity, bias=bias[:]).then_inc(s["qhi"], 1)

            def x_high(b):
                act.wait_ge(s["xT_in"], 16 * (b + 1))
                at_least(act, s["xmm"], LT * b)
                act.copy(xT_hi[:], xT_raw[:]).then_inc(s["xThi"], 1)

            def soft(b, j):
                act.wait_ge(s["nmax"], LT * b + j + 1)
                at_least(act, s["tp"], LT * b)
                act.activation(prob[:, j, :], bank[j % 2][:, :], ACT.Exp, bias=nmx[:, j:j + 1],
                               accum_out=den[:, j:j + 1]).then_inc(s["expd"], 1)

            def normalise(b):
                act.wait_ge(s["rden"], b + 1)
                for j in range(LT):
                    act.activation(prob[:, j, :], prob[:, j, :], ACT.Identity, bias=less_mean[:],
                                   scale=rden[:, j:j + 1]).then_inc(s["prb"], 1)

            def prob_high(b, j):
                at_least(act, s["xmm"], LT * b)
                act.wait_ge(s["tp"], LT * b + j + 1)
                leave(probT_hi[:, :, j * P:(j + 1) * P], j, "probT")

            def ln2_high(b, j):
                if b == 0:
                    act.wait_ge(s["split_lo"], 1)
                at_least(act, s["sup"], IT * b)
                act.wait_ge(s["t2"], LT * b + j + 1)
                leave(lnT_hi[:, :, j * P:(j + 1) * P], j, "lnThi")

            def gate_shared(b, c):
                n = IT * b + c
                m = KI[ORDER[c]]
                act.wait_ge(s["sgate"], n + 1)
                at_least(act, s["hlo"], n - 1)
                act.activation(sig[0:m, n % 2, :], bank[0 if c == 1 else 2][0:m, :], ACT.Sigmoid).then_inc(s["sigd"], 1)

            def hidden_high(b, c):
                n = IT * b + c
                m = KI[ORDER[c]]
                act.wait_ge(s["hid"], n + 1)
                at_least(act, s["dm"], LT * b)
                if n == 0:
                    act.wait_ge(s["split_lo"], 1 + IT)
                act.copy(hT_hi[0:m, ORDER[c], :], sig[0:m, n % 2, :]).then_inc(s["hhi"], 1)

            def logits_out(b):
                m = KI[IT - 1]
                act.wait_ge(s["sup"], IT * b + 1)
                at_least(act, s["lgT"], b)
                act.copy(lgT[:], bank[3][m:m + E, :]).then_inc(s["lgcopy"], 1)

            def add_ln2(b):
                act.wait_ge(s["coef"], b + 1)
                act.wait_ge(s["ln2"], LT * (b + 1))
                for j in range(LT):
                    t = LT * b + j
                    act.activation(acc[:, t, :], acc[:, t, :], ACT.Identity, bias=drop[:, j:j + 1],
                                   scale=grow[:, j:j + 1]).then_inc(s["base"], 1)

            act.wait_ge(s["small_in"], 16 * 4)
            act.activation(tg[:, 0:2], g_sb[:], ACT.Tanh).then_inc(s["gates"], 1)
            act.activation(tg[:, 2:3], g_sb[:, 1:2], ACT.Tanh, scale=-1.0).then_inc(s["gates"], 1)
            qk(0)
            x_high(0)
            for j in range(LT):
                soft(0, j)
            act.wait_ge(s["const"], CONSTS)
            normalise(0)
            for j in range(LT):
                prob_high(0, j)
            act.wait_ge(s["sgu_in"], 16)
            act.copy(sgu_hi[:], sgu_raw[:]).then_inc(s["split_hi"], 1)
            act.wait_ge(s["sd_in"], 16 * IT)
            for k in range(IT):
                act.copy(sd_hi[0:KI[k], k, :], sd_raw[0:KI[k], k, :]).then_inc(s["split_hi"], 1)
            for b in range(NB):
                more = b < last_b
                if more:
                    x_high(b + 1)
                    qk(b + 1)
                ln2_high(b, 0)
                if more:
                    soft(b + 1, 0)
                ln2_high(b, 1)
                if more:
                    soft(b + 1, 1)
                ln2_high(b, 2)
                ln2_high(b, 3)
                if more:
                    soft(b + 1, 2)
                    soft(b + 1, 3)
                logits_out(b)
                if more:
                    normalise(b + 1)
                gate_shared(b, 0)
                act.wait_ge(s["lgshift"], b + 1)
                act.activation(rexp_sb[:], ra[0][:], ACT.Exp).then_inc(s["rexp"], 1)
                hidden_high(b, 0)
                gate_shared(b, 1)
                add_ln2(b)
                if more:
                    prob_high(b + 1, 0)
                hidden_high(b, 1)
                if more:
                    prob_high(b + 1, 1)
                gate_shared(b, 2)
                if more:
                    prob_high(b + 1, 2)
                    prob_high(b + 1, 3)
                hidden_high(b, 2)

            def sigmoid(u, v):
                act.wait_ge(s["cgu"], u + 1)
                at_least(act, s["ch"], u - 1)
                act.activation(sigc[:, v, :], bank[2 * v][:, 0:I], ACT.Sigmoid).then_inc(s["csig"], 1)

            def hidden_out(u, v):
                act.wait_ge(s["ct"], u + 1)
                at_least(act, s["cy"], u - 1)
                act.copy(hTb[:, v], bankHT[:, 0:IT * P].rearrange("p (k l) -> p k l", k=IT)).then_inc(s["cev"], 1)

            def step(q, r):
                u = SLOTS * q + r
                known = isinstance(u, int)
                if not known or 1 <= u <= NE:
                    sigmoid(u - 1, (r - 1) % 2)
                if not known or 2 <= u <= NE + 1:
                    hidden_out(u - 2, r % 2)

            for r in range(SLOTS):
                step(0, r)
            with act.Fori(1, QN) as q:
                for r in range(SLOTS):
                    step(q, r)
            for u in range(SLOTS * QN, NE + 2):
                step(u // SLOTS, u % SLOTS)

        @block.vector
        def _(dve):
            V = nc.vector
            chain = [0]

            def link(ins):
                chain[0] += 1
                ins.then_inc(s["dchain"], 1)
                dve.wait_ge(s["dchain"], chain[0])

            def statistics(rows, n, b, j):
                link(V.bn_stats(out=st[n][:, j, :], in_=rows))
                V.bn_aggr(out=mv[n][:, j, :], in_=st[n][:, j, :]).then_inc(s[f"stat{n + 1}"], 1)

            def variance(n, b):
                dve.wait_ge(s[f"stat{n + 1}"], LT * (b + 1))
                V.tensor_scalar(ve[n][:], mv[n][:, :, 1], EPS, None, ALU.add).then_inc(s[f"var{n + 1}"], 1)

            def ln1_stats(b):
                dve.wait_ge(X_IN[b], 16)
                for j in range(LT):
                    statistics(acc[:, LT * b + j, :], 0, b, j)
                variance(0, b)

            def qk_low(b):
                for n, (dst, hi, bias) in enumerate(((q_lo, q_hi, bq_sb), (k_lo, k_hi, bk_sb))):
                    dve.wait_ge(s["qhi"], 2 * b + n + 1)
                    V.scalar_tensor_tensor(out=dst[:], in0=bank[n][:, :], scalar=bias[:], in1=hi[:].bitcast(F32),
                                           op0=ALU.add, op1=ALU.subtract).then_inc(s["qlo"], 1)

            def row_max(b, j):
                dve.wait_ge(s["eng"], LT * b + j + 1)
                V.tensor_reduce(nmx[:, j:j + 1], bank[j % 2][:, :], AX.X, ALU.max, negate=True).then_inc(s["nmax"], 1)

            def over_sums(b):
                dve.wait_ge(s["expd"], LT * (b + 1))
                at_least(dve, s["prb"], LT * b)
                V.reciprocal(rden[:], den[:]).then_inc(s["rden"], 1)

            def residual(b):
                dve.wait_ge(s["rstd1"], b + 1)
                for j in range(LT):
                    t = LT * b + j
                    dve.wait_ge(s["xmm"], t + 1)
                    V.scalar_tensor_tensor(out=acc[:, t, :], in0=bank[6 + j % 2][:, :], scalar=rs[0][:, j:j + 1],
                                           in1=acc[:, t, :], op0=ALU.mult, op1=ALU.add).then_inc(s["x1"], 1)
                    dve.wait_ge(s["x1"], t + 1)
                    statistics(acc[:, t, :], 1, b, j)

            def ln2_apply(b):
                variance(1, b)
                dve.wait_ge(s["rstd2"], b + 1)
                at_least(dve, s["t2"], LT * b)
                at_least(dve, s["rowsb"], b)
                for j in range(LT):
                    t = LT * b + j
                    V.tensor_scalar(lnr2[:, j, :], acc[:, t, :], mv[1][:, j, 0:1], rs[1][:, j:j + 1],
                                    ALU.subtract, ALU.mult).then_inc(s["ln2"], 1)

            def low(dst, hi, b, done_hi, done_lo, j):
                tok = slice(j * P, (j + 1) * P)
                dve.wait_ge(s[done_hi], LT * b + j + 1)
                V.tensor_tensor(dst[:, :, tok], bank[4 + j % 2][:, :].rearrange("p (k l) -> p k l", k=NT),
                                hi[:, :, tok].bitcast(F32), ALU.subtract).then_inc(s[done_lo], 1)

            def prob_low(b, j):
                at_least(dve, s["xmm"], LT * b)
                low(probT_lo, probT_hi, b, "probT", "probTlo", j)

            def ln2_low(b, j):
                at_least(dve, s["sup"], IT * b)
                if b == 0:
                    dve.wait_ge(s["split_lo"], 1)
                low(lnT_lo, lnT_hi, b, "lnThi", "lnTlo", j)

            def over_e(v):
                return v.rearrange("p (j a) -> p j a", a=1).to_broadcast([P, v.shape[1], E])

            def choose(b):
                lg = bank[7][:, 0:LT * E].rearrange("p (j e) -> p j e", e=E)
                dve.wait_ge(s["lgT"], b + 1)
                link(V.tensor_reduce(rv[0][:], lg, AX.X, ALU.max))
                V.tensor_tensor(ra[0][:], lg, over_e(rv[0][:]), ALU.subtract).then_inc(s["lgshift"], 1)
                dve.wait_ge(s["rexp"], b + 1)
                link(V.tensor_reduce(rv[1][:], rexp_sb[:], AX.X, ALU.add))
                link(V.reciprocal(rv[2][:], rv[1][:]))
                link(V.tensor_tensor(ra[1][:], rexp_sb[:], over_e(rv[2][:]), ALU.mult))
                for c in range(TOP):
                    top = cw[:, c, :]
                    link(V.tensor_reduce(top, ra[1][:], AX.X, ALU.max))
                    link(V.tensor_tensor(ra[2][:], ra[1][:], over_e(top), ALU.is_equal))
                    link(V.tensor_tensor(ra[2][:], ra[2][:], down_idx[:], ALU.mult))
                    link(V.tensor_reduce(rv[0][:], ra[2][:], AX.X, ALU.max))
                    link(V.tensor_tensor(mask[c][:], down_idx[:], over_e(rv[0][:]), ALU.is_equal))
                    if c == 0:
                        link(V.scalar_tensor_tensor(out=ra[1][:], in0=mask[c][:], scalar=-2.0, in1=ra[1][:],
                                                    op0=ALU.mult, op1=ALU.add))
                if b:
                    dve.wait_ge(s["scat"], 16 * TOP * LT * b)
                link(V.tensor_scalar(cwg[:], cw[:], tg[:, 1:2], None, ALU.mult))
                V.tensor_tensor(picked[:], mask[0][:], mask[1][:], ALU.add).then_inc(s["pick"], 1)

            def places(b):
                dve.wait_ge(s["rank"], b + 1)
                totals = bank[6][:, LT * E:2 * LT * E].rearrange("p (j e) -> p e j", e=E)
                link(V.tensor_copy(tot[:], totals))
                flat = lambda v: v[:].rearrange("p e j -> p (e j)")
                link(V.tensor_tensor_scan(flat(upto), flat(reset), flat(tot), 0.0, ALU.mult, ALU.add))
                link(V.tensor_tensor(before[:], upto[:], tot[:], ALU.subtract))
                link(V.tensor_tensor(before[:], before[:],
                                     filled[:, 0:E].rearrange("p (e a) -> p e a", a=1).to_broadcast([P, E, LT]), ALU.add))
                link(V.tensor_tensor(filled[:, 0:E], filled[:, 0:E], upto[:, :, LT - 1], ALU.add))
                V.tensor_tensor(ra[0][:], bank[6][:, 0:LT * E].rearrange("p (j e) -> p j e", e=E),
                                before[:].rearrange("p e j -> p j e"), ALU.add).then_inc(s["place"], 1)
                dve.wait_ge(s["place"], b + 1)
                for c in range(TOP):
                    link(V.tensor_tensor(ra[2][:], mask[c][:], ra[0][:], ALU.mult))
                    link(V.tensor_reduce(rv[c][:], ra[2][:], AX.X, ALU.add))
                at_least(dve, s["scat"], 16 * TOP * LT * b)
                link(V.tensor_copy(slot[:, 0, :], rv[0][:]))
                V.tensor_copy(slot[:, 1, :], rv[1][:]).then_inc(s["placed"], 1)

            def tables():
                link(V.tensor_tensor(cnt[:], filled[:, 0:E], region0[:], ALU.subtract))
                link(V.tensor_tensor(ahead[:], filled[:, 1:E + 1], filled[:, 0:E], ALU.subtract))
                parts = big[:].rearrange("p t e -> p (t e)")[:, 0:E * TT].rearrange("p (e j) -> p e j", e=E)
                link(V.tensor_tensor(parts, cnt[:].rearrange("p (e a) -> p e a", a=1).to_broadcast([P, E, TT]),
                                     fill_at[:].rearrange("p (a j) -> p a j", a=1).to_broadcast([P, E, TT]), ALU.is_gt))
                link(V.tensor_reduce(ntile[:], parts, AX.X, ALU.add))
                link(V.tensor_tensor_scan(tend[:], ones[:, 0:E], ntile[:], 0.0, ALU.mult, ALU.add))
                link(V.tensor_scalar(skip[:], ntile[:], -float(P), float(REG), ALU.mult, ALU.add))
                across = lambda v: v[:].rearrange("p (a e) -> p a e", a=1).to_broadcast([P, NE, E])
                start = big[:, 0:NE]
                link(V.tensor_tensor(start, over_e(tile_no[:]), across(tend), ALU.is_ge))
                link(V.memset(etab[:], 0.0))
                link(V.tensor_reduce(tf[:], start, AX.X, ALU.add))
                link(V.tensor_scalar(etab[:, SLOTS:SLOTS + NE], tf[:], float(E - 1), None, ALU.min))
                steps = etab[:].rearrange("p (q r) -> p q r", r=SLOTS)
                link(V.tensor_scalar(epack[0][:], steps[:, 0:NQ, 1], 1.0, None, ALU.mult))
                for i in range(1, 2 * SLOTS - 1):
                    a = (1 + i) // SLOTS
                    link(V.scalar_tensor_tensor(out=epack[i % 2][:], in0=steps[:, a:a + NQ, (1 + i) % SLOTS], scalar=float(E ** i),
                                                in1=epack[(i + 1) % 2][:], op0=ALU.mult, op1=ALU.add))
                link(V.tensor_copy(epack_i[:], epack[0][:]))
                link(V.tensor_tensor(big2[:], start, across(ahead), ALU.mult))
                link(V.tensor_reduce(limit[:], big2[:], AX.X, ALU.add))
                link(V.tensor_scalar(limit[:], limit[:], filled[:, 0:1], -float(P), ALU.add, ALU.add))
                link(V.tensor_tensor(start, start, across(skip), ALU.mult))
                link(V.tensor_reduce(tf[:], start, AX.X, ALU.add))
                link(V.scalar_tensor_tensor(out=tf[:], in0=tile_no[:], scalar=float(P), in1=tf[:],
                                            op0=ALU.mult, op1=ALU.add))
                link(V.tensor_scalar(tf[:], tf[:], float(P), None, ALU.add))
                link(V.tensor_tensor(over[:], tf[:], limit[:], ALU.subtract))
                link(V.scalar_tensor_tensor(out=again[:], in0=over[:], scalar=part[:], in1=unused_at[:],
                                            op0=ALU.is_gt, op1=ALU.mult))
                link(V.tensor_tensor(tf[:], tf[:], limit[:], ALU.min))
                V.tensor_copy(erow[:], tf[:]).then_inc(s["tabs"], 1)

            def shared_hidden(b, c):
                n = IT * b + c
                m = KI[ORDER[c]]
                dve.wait_ge(s["sigd"], n + 1)
                dve.wait_ge(s["sup"], n + 1)
                V.tensor_tensor(sig[0:m, n % 2, :], sig[0:m, n % 2, :], bank[1 if c == 1 else 3][0:m, :], ALU.mult).then_inc(s["hid"], 1)

            def shared_out(b):
                for j in range(LT):
                    t = LT * b + j
                    dve.wait_ge(s["dm"], t + 1)
                    dve.wait_ge(s["base"], t + 1)
                    V.scalar_tensor_tensor(out=acc[:, t, :], in0=bank[6 + j % 2][:, :], scalar=tg[:, 1:2],
                                           in1=acc[:, t, :], op0=ALU.mult, op1=ALU.add).then_inc(s["shared"], 1)

            dve.wait_ge(s["small_in"], 16 * 4)
            qk_low(0)
            for j in range(LT):
                row_max(0, j)
            ln1_stats(0)
            over_sums(0)
            dve.wait_ge(s["const"], CONSTS)
            dve.wait_ge(s["gates"], 2)
            for j in range(LT):
                prob_low(0, j)
            for b in range(NB):
                more = b < last_b
                residual(b)
                ln2_apply(b)
                if more:
                    qk_low(b + 1)
                if b:
                    shared_out(b - 1)
                if more:
                    row_max(b + 1, 0)
                ln2_low(b, 0)
                ln2_low(b, 1)
                if more:
                    row_max(b + 1, 1)
                ln2_low(b, 2)
                ln2_low(b, 3)
                if more:
                    row_max(b + 1, 2)
                    row_max(b + 1, 3)
                    ln1_stats(b + 1)
                    over_sums(b + 1)
                shared_hidden(b, 0)
                choose(b)
                shared_hidden(b, 1)
                if more:
                    prob_low(b + 1, 0)
                    prob_low(b + 1, 1)
                places(b)
                if more:
                    prob_low(b + 1, 2)
                    prob_low(b + 1, 3)
                shared_hidden(b, 2)
            tables()
            shared_out(last_b)
            link(V.memset(hrow[:, :, I:IT * P], 0.0))

            def rows_out(u, r):
                dve.wait_ge(s["cxt"], u + 1)
                at_least(dve, s["cgu"], u - 1)
                V.tensor_tensor(dest[:, bass.ds(u, 1)], xt[:, r, DST:DST + 1], again[:, bass.ds(u, 1)], ALU.max)
                V.tensor_copy(wt[:, bass.ds(u, 1)], xt[:, r, WT:WT + 1])
                V.tensor_copy(xTb[:, r % 2], bankXT[:, 0:N].rearrange("p (k l) -> p k l", k=NT)).then_inc(s["xev"], 1)

            def hidden(u, v):
                dve.wait_ge(s["csig"], u + 1)
                at_least(dve, s["ct"], u - 1)
                V.tensor_tensor(hrow[:, v, 0:I], sigc[:, v, :], bank[2 * v + 1][:, 0:I], ALU.mult).then_inc(s["ch"], 1)

            def result(u, v, slot_, q):
                dve.wait_ge(s["cy"], u + 1)
                if not isinstance(q, int) or q > 0:
                    dve.wait_ge(s_yd[slot_], 16 * q)
                V.tensor_scalar(ysb[:, slot_, :], bank[6 + v][:, :], wt[:, bass.ds(u, 1)].bitcast(F32), None,
                                ALU.mult).then_inc(s["yev"], 1)

            def step(q, r):
                u = SLOTS * q + r
                known = isinstance(u, int)
                if not known or 1 <= u <= NE:
                    hidden(u - 1, (r - 1) % 2)
                if not known or 3 <= u:
                    result(u - 3, (r - 3) % 2, (r - 3) % SLOTS, q if r == 3 else q - 1)
                if not known or u + 1 < NE:
                    rows_out(u + 1, (r + 1) % SLOTS)

            rows_out(0, 0)
            for q in range(2):
                for r in range(SLOTS):
                    step(q, r)
            with dve.Fori(2, QN) as q:
                for r in range(SLOTS):
                    step(q, r)
            for u in range(SLOTS * QN, NE + 3):
                step(u // SLOTS, u % SLOTS)

            for t in range(TT):
                dve.wait_ge(s["zsum"], t + 1)
                V.tensor_tensor(acc[:, t, :], bank[t % 4][:, :], acc[:, t, :], ALU.add).then_inc(s["comb"], 1)


def kernel(x, ctx_1024, g_xattn, g_ffn, L0_xattn_Wq, L0_xattn_bq, L0_xattn_Wk, L0_xattn_bk, L0_ffn_router_w,
           L0_ffn_shared_gate, L0_ffn_shared_up, L0_ffn_shared_down, L0_ffn_w_gate, L0_ffn_w_up, L0_ffn_w_down):
    import numpy as np
    import concourse.bacc as bacc
    from concourse import mybir as mb
    from concourse.bass_utils import run_bass_kernel_spmd

    T = lambda a: np.asarray(a).swapaxes(-1, -2)
    arrays = {
        "x": x, "xT": T(x), "ctxT": T(ctx_1024), "g2": np.stack([np.asarray(g_xattn), np.asarray(g_ffn)]),
        "wqT": T(L0_xattn_Wq), "wkT": T(L0_xattn_Wk), "bq": L0_xattn_bq, "bk": L0_xattn_bk,
        "sguT": np.concatenate([T(L0_ffn_shared_gate), T(L0_ffn_shared_up), T(L0_ffn_router_w)], 1),
        "sdT": T(L0_ffn_shared_down),
        "wguT": np.concatenate([T(L0_ffn_w_gate), T(L0_ffn_w_up)], 2), "wdT": T(L0_ffn_w_down),
    }
    arrays = {n: np.ascontiguousarray(a) for n, a in arrays.items()}
    nc = bacc.Bacc("TRN2", target_bir_lowering=False, num_devices=1)
    args = [nc.dram_tensor(n, a.shape, mb.dt.from_np(a.dtype), kind="ExternalInput").ap() for n, a in arrays.items()]
    shape = np.asarray(x).shape
    o = nc.dram_tensor("out", (shape[0] * shape[1], shape[2]), mb.dt.float32, kind="ExternalOutput").ap()
    gated_block(nc, *args, o)
    r = run_bass_kernel_spmd(nc, [arrays], core_ids=[0])
    return np.asarray(r.results[0]["out"]).reshape(shape)
```

```python
from contextlib import ExitStack

import concourse.bass as bass
from concourse import mybir

ALU = mybir.AluOpType
ACT = mybir.ActivationFunctionType
AX = mybir.AxisListType
F32 = mybir.dt.float32
F32R = mybir.dt.float32r
BF16 = mybir.dt.bfloat16
U32 = mybir.dt.uint32

P = 128
EPS = 1e-5
TAKEN = 1e30
TOP = 2


def at_least(eng, sem, n):
    if not isinstance(n, int) or n > 0:
        eng.wait_ge(sem, n)


def gated_block(nc, x, xT, ctxT, g2, wqT, wkT, bq, bk, sguT, sdT, wguT, wdT, out):
    NB, L, N = x.shape
    C = ctxT.shape[1]
    D = wqT.shape[1]
    E = wguT.shape[0]
    I = sdT.shape[0]
    LT, NT, CT = L // P, N // P, C // P
    KI = [P, P, I - 2 * P]
    IT = len(KI)
    TT = NB * LT
    TOK = TT * P
    ROW = N // 2 + 2
    DST, WT = N // 2, N // 2 + 1
    GU = 2 * I + E
    REG = P + TOK
    NE = (TOK * TOP + (P - 1) * E) // P
    SLOTS = 4
    ZS = 12
    QN = NE // SLOTS
    NQ = (NE + 2) // SLOTS + 1
    last_b = NB - 1
    ORDER = [IT - 1] + list(range(IT - 1))

    xg = nc.dram_tensor("xg", (E * REG + P, ROW), U32, kind="Internal").ap()
    z = nc.dram_tensor("z", (TOP * TOK + NE * P, N), BF16, kind="Internal").ap()

    with ExitStack() as ctx:
        def sb(name, shape, dt=F32):
            return ctx.enter_context(nc.sbuf_tensor(name, shape, dt))

        def sem(name):
            return ctx.enter_context(nc.semaphore(name))

        bank = [ctx.enter_context(nc.psum_tensor(f"bank{i}", [P, 512], F32)) for i in range(8)]
        bankXT = bank[4][:, :].bitcast(BF16)
        bankHT = bank[5][:, :].bitcast(BF16)

        bq_sb = sb("bq_sb", [P, 1])
        bk_sb = sb("bk_sb", [P, 1])
        g_sb = sb("g_sb", [P, 2])
        tg = sb("tg", [P, 3])
        less_mean = sb("less_mean", [P, 1])
        ones = sb("ones", [P, P])
        ident = sb("ident", [P, P])
        identb = sb("identb", [P, P], BF16)
        tri = sb("tri", [P, P])
        half = sb("half", [P, LT])
        down_idx = sb("down_idx", [P, LT, E])
        reset = sb("reset", [P, E, LT])
        region0 = sb("region0", [P, E])
        part = sb("part", [P, 1])
        unused_at = sb("unused_at", [P, NE])
        fill_at = sb("fill_at", [P, TT])
        tile_no = sb("tile_no", [P, SLOTS * NQ])
        tile_row = sb("tile_row", [P, NE])
        st = [sb(f"st{i}", [P, LT, 6]) for i in range(2)]
        mv = [sb(f"mv{i}", [P, LT, 2]) for i in range(2)]
        ve = [sb(f"ve{i}", [P, LT]) for i in range(2)]
        rs = [sb(f"rs{i}", [P, LT]) for i in range(2)]
        grow = sb("grow", [P, LT])
        drop = sb("drop", [P, LT])
        nmx = sb("nmx", [P, LT])
        den = sb("den", [P, LT])
        rden = sb("rden", [P, LT])
        lgT = sb("lgT", [E, L])
        ra = [sb(f"ra{i}", [P, LT, E]) for i in range(3)]
        shifted = sb("shifted", [P, LT, E + 1])
        rexp_sb = sb("rexp_sb", [P, LT, E + 1])
        mask = [sb(f"mask{i}", [P, LT, E]) for i in range(TOP)]
        picked = sb("picked", [P, LT, E])
        rv = [sb(f"rv{i}", [P, LT]) for i in range(3)]
        rank_of = sb("rank_of", [P, TOP, LT])
        second = sb("second", [P, TOP, LT])
        token = sb("token", [P, TT])
        tot = sb("tot", [P, E, LT])
        upto = sb("upto", [P, E, LT])
        before = sb("before", [P, E, LT])
        filled = sb("filled", [P, E + 1])
        cwg = sb("cwg", [P, TOP, LT])
        slot = sb("slot", [P, TOP, LT], U32)
        carrier = sb("carrier", [P, LT])
        cnt = sb("cnt", [P, E])
        ntile = sb("ntile", [P, E])
        tend = sb("tend", [P, E])
        skip = sb("skip", [P, E])
        ahead = sb("ahead", [P, E])
        etab = sb("etab", [P, SLOTS * (NQ + 1)])
        powers = sb("powers", [P, 2 * SLOTS - 1])
        epack_i = sb("epack_i", [P, NQ], U32)
        erow = sb("erow", [P, NE], U32)
        padr = sb("padr", [P, ROW], U32)
        again = sb("again", [P, NE], U32)
        sent_i = sb("sent_i", [P, SLOTS], U32)
        dest = sb("dest", [P, NE], U32)
        wt = sb("wt", [P, NE], U32)
        desti = sb("desti", [P, SLOTS], U32)
        lnb = [sb(f"lnb{c}", [P, LT, ROW], U32) for c in range(TOP)]
        warm = sb("warm", [P, 1])
        acc = sb("acc", [P, TT, N])
        KP = NT // 2
        wgu_lo = sb("wgu_lo", [P, KP, E, 2 * I], BF16)

        top = -(-nc.sbuf_base // 32) * 32

        def place(items, start):
            made = []
            for name, shape, dt in items:
                start = -(-start // 32) * 32
                made.append(nc.alloc_sbuf_tensor_at(name, shape, dt, offset=start))
                n = 1
                for d in shape[1:]:
                    n *= d
                start += n * (2 if dt == BF16 else 4)
            assert start <= nc.sbuf_usable_end, (start, nc.sbuf_usable_end)
            return made, start

        (lnT_hi, lnT_lo), lnT_end = place((
            ("lnT_hi", [P, NT, L], F32R), ("lnT_lo", [P, NT, L], F32R)), top)
        (hT_hi, hT_lo), hT_end = place((
            ("hT_hi", [P, IT, L], F32R), ("hT_lo", [P, IT, L], F32R)), lnT_end)
        (sig,), sig_end = place((("sig", [P, 2, L], F32),), hT_end)
        (sgu_hi, sgu_lo, sd_hi, sd_lo), att = place((
            ("sgu_hi", [P, NT, GU], F32R), ("sgu_lo", [P, NT, GU], F32R),
            ("sd_hi", [P, IT, N], F32R), ("sd_lo", [P, IT, N], F32R)), sig_end)
        (xT_raw, cx, wq_sb, wk_sb, q_hi, q_lo, k_hi, k_lo, prob, xT_hi, xT_lo, probT_hi, probT_lo, lnr2), _end = place((
            ("xT_raw", [P, NT, L], F32), ("cx", [P, CT, L], F32), ("wq_sb", [P, CT, D], F32), ("wk_sb", [P, CT, D], F32),
            ("q_hi", [P, L], F32R), ("q_lo", [P, L], F32R), ("k_hi", [P, L], F32R), ("k_lo", [P, L], F32R),
            ("prob", [P, LT, L], F32), ("xT_hi", [P, NT, L], F32R), ("xT_lo", [P, NT, L], F32R),
            ("probT_hi", [P, NT, L], F32R), ("probT_lo", [P, NT, L], F32R), ("lnr2", [P, LT, N], F32)), att)
        (sgu_raw,), _ = place((("sgu_raw", [P, NT, GU], F32),), top)
        (sd_raw,), _ = place((("sd_raw", [P, IT, N], F32),), lnT_end)
        (xt, xTb, hrow, hTb, sigc, ysb), c_end = place((
            ("xt", [P, SLOTS, ROW], U32), ("xTb", [P, 2, NT, P], BF16), ("hrow", [P, 2, IT * P], BF16),
            ("hTb", [P, 2, IT, P], BF16), ("sigc", [P, 2, I], F32), ("ysb", [P, SLOTS, N], BF16)), top)
        assert c_end <= lnT_end
        (zb,), z_end = place((("zb", [P, ZS, N], BF16),), lnT_end)
        assert z_end <= hT_end
        (za,), za_end = place((("za", [P, TT, N], BF16),), sig_end)
        assert za_end <= att
        (wgu_hi, wd_sb), w_end = place((
            ("wgu_hi", [P, NT - KP, E, 2 * I], BF16), ("wd_sb", [P, IT, E, N], BF16)), att)
        (epack, slot_rows, slot_sum, tf, digits, big, big2, limit, over), big_end = place((
            ("epack", [P, NQ], F32), ("slot_rows", [P, SLOTS, NQ], F32), ("slot_sum", [P, SLOTS], F32),
            ("tf", [P, NE], F32),
            ("digits", [P, NQ, 2 * SLOTS - 1], F32),
            ("big", [P, max(NE, TT), E], F32), ("big2", [P, NE, E], F32), ("limit", [P, NE], F32), ("over", [P, NE], F32)), w_end)
        assert big_end <= _end
        xtb = xt[:].rearrange("p s r -> p (s r)").bitcast(BF16).rearrange("p (s r) -> p s r", s=SLOTS)

        lnb_rows = [v[:].rearrange("p j r -> p (j r)").bitcast(BF16).rearrange("p (j r) -> p j r", j=LT)[:, :, 0:N] for v in lnb]

        def wgu(k, e, lo, n):
            return wgu_lo[:, k, e, lo:lo + n] if k < KP else wgu_hi[:, k - KP, e, lo:lo + n]

        s = {n: sem(n) for n in (
            "ctx_in w_in small_in sgu_in sd_in wgu_in wgu2_in wd_in const gates split_hi split_lo "
            "stat1 var1 rstd1 stat2 var2 rstd2 coef ln2 proj qhi qlo t2 lnThi lnTlo xThi xTlo probT probTlo eng nmax expd rden prb tp "
            "xmm x1 base lgcopy lgT lgshift rexp pick order weight rank place placed scat rowsb rowsb2 sgate sup sigd hid hhi hlo dm shared "
            "sent packed xT_in padrows padout tabs cxt xev cgu csig ch ct cev cy yev dchain pchain didx za_in zsum comb outd").split()}
        s_xl = [sem(f"xt_in{i}") for i in range(SLOTS)]
        s_yd = [sem(f"y_out{i}") for i in range(SLOTS)]
        s_zl = [sem(f"z_in{i}") for i in range(ZS)]
        X_IN = [sem(f"x_in{b}") for b in range(NB)]

        QK_BANK = [2 if b == 1 else 0 for b in range(NB)]
        CONSTS = 18 + 2 * SLOTS - 1

        block = ctx.enter_context(nc.Block())

        @block.sync
        def _(sp):
            def load_x(b):
                sp.dma_start(acc[:, LT * b:LT * (b + 1), :], x[b].rearrange("(j p) n -> p j n", p=P)).then_inc(X_IN[b], 16)

            def load_ctx(b):
                sp.dma_start(cx[:], ctxT[b].rearrange("(k p) l -> p k l", p=P)).then_inc(s["ctx_in"], 16)

            def load_xT(b):
                sp.dma_start(xT_raw[:], xT[b].rearrange("(k p) l -> p k l", p=P)).then_inc(s["xT_in"], 16)

            sp.dma_start(wq_sb[:], wqT.rearrange("(k p) d -> p k d", p=P)).then_inc(s["w_in"], 16)
            sp.dma_start(wk_sb[:], wkT.rearrange("(k p) d -> p k d", p=P)).then_inc(s["w_in"], 16)
            load_ctx(0)
            sp.dma_start(bq_sb[:], bq.rearrange("(d a) -> d a", a=1)).then_inc(s["small_in"], 16)
            sp.dma_start(bk_sb[:], bk.rearrange("(d a) -> d a", a=1)).then_inc(s["small_in"], 16)
            for j in range(2):
                sp.dma_start(g_sb[:, j:j + 1], g2[j:j + 1, :].to_broadcast([P, 1])).then_inc(s["small_in"], 16)
            load_xT(0)
            load_x(0)
            sp.wait_ge(s["proj"], 2)
            load_ctx(1)
            sp.dma_start(sgu_raw[:], sguT.rearrange("(k p) i -> p k i", p=P)).then_inc(s["sgu_in"], 16)
            for k in range(IT):
                sp.dma_start(sd_raw[0:KI[k], k, :], sdT[k * P:k * P + KI[k], :]).then_inc(s["sd_in"], 16)
            sp.wait_ge(s["padrows"], 1)
            for e in range(E + 1):
                sp.dma_start(xg[e * REG:e * REG + P, :], padr[:]).then_inc(s["padout"], 16)
            for b in range(1, NB):
                if b > 1:
                    sp.wait_ge(s["proj"], 2 * b)
                    load_ctx(b)
                sp.wait_ge(s["xThi"], b)
                sp.wait_ge(s["xTlo"], b)
                load_xT(b)
                load_x(b)
            sp.wait_ge(s["padout"], 16 * (E + 1))
            sp.wait_ge(s["scat"], 16 * TOP * TT)
            sp.wait_ge(s["tabs"], 1)
            sp.wait_ge(s["sup"], IT * NB)

            def load_tile(u, slot_, free):
                if free is not None:
                    sp.wait_ge(s["xev"], free)
                row = sp.value_load(erow[0:1, bass.ds(u, 1)], min_val=0, max_val=E * REG)
                sp.dma_start(xt[:, slot_, :], xg[bass.ds(row, P), :]).then_inc(s_xl[slot_], 16)

            for r in range(SLOTS):
                load_tile(r, r, None)
            with sp.Fori(1, QN) as q:
                for r in range(SLOTS):
                    load_tile(SLOTS * q + r, r, SLOTS * q + r - SLOTS + 1)
            for u in range(SLOTS * QN, NE):
                load_tile(u, u % SLOTS, u - SLOTS + 1)
            zt = z[0:TOP * TOK, :].rearrange("(c t p) n -> c p t n", c=TOP, p=P)
            sp.wait_ge(s["sent"], 1)
            sent = [sp.value_load(sent_i[0:1, r:r + 1], min_val=16, max_val=16 * len(range(r, NE, SLOTS))) for r in range(SLOTS)]
            for r in range(SLOTS):
                sp.wait_ge(s_yd[r], sent[r])
            for i in range(0, TT, LT):
                sp.dma_start(za[:, i:i + LT], zt[0, :, i:i + LT]).then_inc(s["za_in"], 16)
            sp.wait_ge(s["dm"], TT)
            for r in range(SLOTS):
                sp.wait_ge(s_yd[r], 16 * len(range(r, NE, SLOTS)))

            def store(t):
                sp.wait_ge(s["comb"], t + 1)
                sp.dma_start(out[t * P:(t + 1) * P, :], acc[:, t, :]).then_inc(s["outd"], 16)
            for t in range(TT):
                if t >= ZS:
                    store(t - ZS)
                sp.dma_start(zb[:, t % ZS], zt[1, :, t]).then_inc(s_zl[t % ZS], 16)
            for t in range(TT - ZS, TT):
                store(t)
            sp.wait_ge(s["outd"], 16 * TT)

        @block.gpsimd
        def _(pool):
            nc.gpsimd.memset(ones[:], 1.0).then_inc(s["const"], 1)
            nc.gpsimd.memset(half[:], -0.5).then_inc(s["const"], 1)
            pool.wait_ge(s["const"], 2)
            nc.gpsimd.affine_select(out=ident[:], in_=ones[:], compare_op=ALU.is_equal, fill=0.0, base=0,
                                    pattern=[[-1, P]], channel_multiplier=1).then_inc(s["const"], 1)
            nc.gpsimd.affine_select(out=tri[:], in_=ones[:], compare_op=ALU.is_gt, fill=0.0, base=0,
                                    pattern=[[1, P]], channel_multiplier=-1).then_inc(s["const"], 1)
            pool.wait_ge(s["const"], 4)
            nc.gpsimd.tensor_copy(identb[:], ident[:]).then_inc(s["const"], 1)

            def iota(t, pattern, base, mult=0):
                nc.gpsimd.iota(t, pattern, base=base, channel_multiplier=mult,
                               allow_small_or_imprecise_dtypes=True).then_inc(s["const"], 1)
            iota(down_idx[:], [[0, LT], [-1, E]], E)
            iota(region0[:], [[REG, E]], P)
            iota(filled[:], [[REG, E + 1]], P)
            nc.gpsimd.memset(less_mean[:], -1.0 / N).then_inc(s["const"], 1)
            iota(part[:], [[0, 1]], 0, 1)
            for i in range(2 * SLOTS - 1):
                nc.gpsimd.memset(powers[:, i:i + 1], float(E ** i)).then_inc(s["const"], 1)
            iota(token[:], [[P, TT]], 0, 1)
            iota(unused_at[:], [[P, NE]], TOP * TOK, 1)
            iota(fill_at[:], [[P, TT]], 0)
            iota(tile_no[:], [[1, SLOTS * NQ]], 0)
            iota(tile_row[:], [[P, NE]], P)
            nc.gpsimd.memset(etab[:], 0.0).then_inc(s["const"], 1)
            nc.gpsimd.memset(reset[:, :, 1:LT], 1.0).then_inc(s["const"], 1)
            nc.gpsimd.memset(reset[:, :, 0:1], 0.0).then_inc(s["const"], 1)

            nc.gpsimd.memset(padr[:], 0).then_inc(s["padrows"], 1)

            chain = [0]

            def link(ins):
                chain[0] += 1
                ins.then_inc(s["pchain"], 1)
                pool.wait_ge(s["pchain"], chain[0])

            def gate(c):
                return tg[:, c:c + 1].to_broadcast([P, LT])

            def factor1(b):
                pool.wait_ge(s["var1"], b + 1)
                link(nc.gpsimd.tensor_tensor(rs[0][:], ve[0][:], half[:], ALU.pow))
                nc.gpsimd.tensor_tensor(rs[0][:], rs[0][:], gate(0), ALU.mult).then_inc(s["rstd1"], 1)

            def factors2(b):
                pool.wait_ge(s["var2"], b + 1)
                nc.gpsimd.tensor_tensor(rs[1][:], ve[1][:], half[:], ALU.pow).then_inc(s["rstd2"], 1)
                pool.wait_ge(s["rstd2"], b + 1)
                if b:
                    pool.wait_ge(s["base"], LT * b)
                link(nc.gpsimd.tensor_tensor(grow[:], rs[1][:], gate(1), ALU.mult))
                link(nc.gpsimd.tensor_tensor(grow[:], grow[:], ones[:, 0:LT], ALU.add))
                link(nc.gpsimd.tensor_tensor(drop[:], rs[1][:], gate(2), ALU.mult))
                nc.gpsimd.tensor_tensor(drop[:], drop[:], mv[1][:, :, 0], ALU.mult).then_inc(s["coef"], 1)

            def x_low(b):
                pool.wait_ge(s["xThi"], b + 1)
                at_least(pool, s["xmm"], LT * b)
                nc.gpsimd.tensor_tensor(xT_lo[:], xT_raw[:], xT_hi[:].bitcast(F32), ALU.subtract).then_inc(s["xTlo"], 1)

            pool.wait_ge(s["gates"], 2)
            x_low(0)
            factor1(0)
            pool.wait_ge(s["split_hi"], 1)
            nc.gpsimd.tensor_tensor(sgu_lo[:], sgu_raw[:], sgu_hi[:].bitcast(F32), ALU.subtract).then_inc(s["split_lo"], 1)
            for k in range(KP):
                pool.dma_start(wgu_lo[:, k], wguT[:, k * P:(k + 1) * P, :].rearrange("e p i -> p e i")).then_inc(s["wgu_in"], 16)

            def down_low():
                for k in range(IT):
                    pool.wait_ge(s["split_hi"], 2 + k)
                    nc.gpsimd.tensor_tensor(sd_lo[0:KI[k], k, :], sd_raw[0:KI[k], k, :], sd_hi[0:KI[k], k, :].bitcast(F32),
                                            ALU.subtract).then_inc(s["split_lo"], 1)

            def hidden_low(b, c):
                n = IT * b + c
                m = KI[ORDER[c]]
                pool.wait_ge(s["hhi"], n + 1)
                nc.gpsimd.tensor_tensor(hT_lo[0:m, ORDER[c], :], sig[0:m, n % 2, :], hT_hi[0:m, ORDER[c], :].bitcast(F32),
                                        ALU.subtract).then_inc(s["hlo"], 1)

            def scatter(b, c):
                pool.wait_ge(s["order"], TOP * (b + 1))
                pool.wait_ge(s["placed"], b + 1)
                pool.wait_ge(s["weight"], b + 1)
                link(nc.gpsimd.tensor_copy(lnb[c][:].bitcast(F32)[:, :, WT], cwg[:, c, :]))
                pool.wait_ge(s[("rowsb", "rowsb2")[c]], b + 1)
                for j in range(LT):
                    nc.gpsimd.indirect_dma_start(
                        out=xg, out_offset=bass.IndirectOffsetOnAxis(ap=slot[:, c, j:j + 1], axis=0),
                        in_=lnb[c][:, j, :], in_offset=None).then_inc(s["scat"], 16)

            for b in range(NB):
                if b == last_b:
                    pool.wait_ge(s["tp"], TT)
                    pool.wait_ge(s["eng"], TT)
                    for k in range(KP, NT):
                        pool.dma_start(wgu_hi[:, k - KP], wguT[:, k * P:(k + 1) * P, :].rearrange("e p i -> p e i")).then_inc(s["wgu2_in"], 16)
                factors2(b)
                if 0 < b < last_b:
                    factor1(b + 1)
                if b == last_b:
                    pool.wait_ge(s["xmm"], TT)
                    for k in range(IT):
                        pool.dma_start(wd_sb[0:KI[k], k], wdT[:, k * P:k * P + KI[k], :].rearrange("e p n -> p e n")).then_inc(s["wd_in"], 16)
                pool.wait_ge(s["ln2"], LT * (b + 1))
                if b:
                    pool.wait_ge(s["scat"], 16 * TOP * LT * b)
                nc.gpsimd.tensor_copy(lnb_rows[0], lnr2[:]).then_inc(s["rowsb"], 1)
                if b == 0:
                    down_low()
                    pool.wait_ge(s["padout"], 16 * (E + 1))
                if b < last_b:
                    x_low(b + 1)
                if b == 0:
                    factor1(1)
                if b < last_b:
                    hidden_low(b, 0)
                    hidden_low(b, 1)
                scatter(b, 0)
                if b < last_b:
                    hidden_low(b, 2)
                scatter(b, 1)

            def send(u, r, q):
                pool.wait_ge(s["yev"], u + 1)
                if q is not None:
                    pool.wait_ge(s_yd[r], 16 * q)
                if isinstance(u, int) and u >= SLOTS * QN:
                    nc.gpsimd.indirect_dma_start(
                        out=z, out_offset=bass.IndirectOffsetOnAxis(ap=dest[:, u:u + 1], axis=0),
                        in_=ysb[:, r, :], in_offset=None).then_inc(s_yd[r], 16)
                    return
                nc.gpsimd.tensor_copy(desti[:, r:r + 1], dest[:, bass.ds(u, 1)]).then_inc(s["didx"], 1)
                pool.wait_ge(s["didx"], u + 1)
                nc.gpsimd.tensor_tensor(carrier[:], half[:], half[:], ALU.add)
                nc.gpsimd.indirect_dma_start(
                    out=z, out_offset=bass.IndirectOffsetOnAxis(ap=desti[:, r:r + 1], axis=0),
                    in_=ysb[:, r, :], in_offset=None).then_inc(s_yd[r], 16)

            for r in range(SLOTS):
                send(r, r, None)
            with pool.Fori(1, QN) as q:
                for r in range(SLOTS):
                    send(SLOTS * q + r, r, q)
            for u in range(SLOTS * QN, NE):
                send(u, u % SLOTS, QN)

        @block.tensor
        def _(pe):
            def turn(src, n):
                for k in range(NT):
                    mm = pe.transpose(bank[4 + n % 2][:, k * P:(k + 1) * P], src[:, k * P:(k + 1) * P], ident[:])
                return mm

            def three(dst, a_hi, a_lo, b_hi, b_lo, first, last_):
                pe.matmul(dst, a_lo, b_hi, start=first, stop=False)
                pe.matmul(dst, a_hi, b_lo, start=False, stop=False)
                return pe.matmul(dst, a_hi, b_hi, start=False, stop=last_)

            def project(b, n):
                w = (wq_sb, wk_sb)[n]
                pe.wait_ge(s["ctx_in"], 16 * (b + 1))
                if b > 1:
                    pe.wait_ge(s["hid"], IT * (b - 2) + 2)
                for k in range(CT):
                    mm = pe.matmul(bank[QK_BANK[b] + n][:, :], w[:, k, :], cx[:, k, :], start=(k == 0), stop=(k == CT - 1))
                mm.then_inc(s["proj"], 1)

            def energy(b, j):
                if j < 2:
                    pe.wait_ge(s["qlo"], 2 * (b + 1))
                    if b == 1:
                        pe.wait_ge(s["expd"], LT)
                else:
                    pe.wait_ge(s["expd"], LT * b + j - 1)
                tok = slice(j * P, (j + 1) * P)
                three(bank[j % 2][:, :], q_hi[:, tok], q_lo[:, tok], k_hi[:], k_lo[:], True, True).then_inc(s["eng"], 1)

            def turn_prob(b, j):
                pe.wait_ge(s["prb"], LT * b + j + 1)
                if j >= 2:
                    pe.wait_ge(s["probTlo"], LT * b + j - 1)
                elif b:
                    pe.wait_ge(s["lnTlo"], LT * (b - 1) + j + 3)
                turn(prob[:, j], j).then_inc(s["tp"], 1)

            def mix(b):
                pe.wait_ge(s["probTlo"], LT * (b + 1))
                pe.wait_ge(s["xTlo"], b + 1)
                for j in range(LT):
                    if j >= 2:
                        pe.wait_ge(s["x1"], LT * b + j - 1)
                    elif b:
                        pe.wait_ge(s["place"], b)
                    for k in range(NT):
                        mm = three(bank[6 + j % 2][:, :], xT_hi[:, k, j * P:(j + 1) * P], xT_lo[:, k, j * P:(j + 1) * P],
                                   probT_hi[:, k, :], probT_lo[:, k, :], k == 0, k == NT - 1)
                    mm.then_inc(s["xmm"], 1)

            def turn_ln2(b, j):
                pe.wait_ge(s["ln2"], LT * b + j + 1)
                if j >= 2:
                    pe.wait_ge(s["lnTlo"], LT * b + j - 1)
                else:
                    pe.wait_ge(s["probTlo"], LT * b + j + 3)
                turn(lnr2[:, j], j).then_inc(s["t2"], 1)

            def turn_logits(b):
                pe.wait_ge(s["lgcopy"], b + 1)
                if b:
                    pe.wait_ge(s["shared"], LT * b)
                else:
                    pe.wait_ge(s["x1"], LT)
                for j in range(LT):
                    mm = pe.transpose(bank[7][:, j * E:(j + 1) * E], lgT[:, j * P:(j + 1) * P], ident[0:E, 0:E])
                mm.then_inc(s["lgT"], 1)

            def rank(b):
                pe.wait_ge(s["pick"], b + 1)
                sel = picked[:].rearrange("p j e -> p (j e)")
                pe.matmul(bank[6][:, 0:LT * E], tri[:], sel, start=True, stop=True)
                pe.matmul(bank[6][:, LT * E:2 * LT * E], ones[:], sel, start=True, stop=True).then_inc(s["rank"], 1)

            def wide_shared(b, c, half_):
                n = IT * b + c
                row = ORDER[c]
                m = KI[row] + (E if half_ and row == IT - 1 else 0)
                free, done = (("sigd", "sgate"), ("hid", "sup"))[half_]
                pair = 0 if c == 1 else 2
                if n == 0:
                    pe.wait_ge(s["split_lo"], 1)
                pe.wait_ge(s["lnTlo"], LT * (b + 1))
                if c == 0:
                    at_least(pe, s[free], IT * b)
                elif c == 1:
                    pe.wait_ge(s["expd"], min(LT * (b + 2), TT))
                else:
                    pe.wait_ge(s[free], IT * b + 1)
                o_ = half_ * I + row * P
                for k in range(NT):
                    if c == 0 and half_ == 0 and k == NT // 2:
                        turn_logits(b)
                    mm = three(bank[pair + half_][0:m, :], sgu_hi[:, k, o_:o_ + m], sgu_lo[:, k, o_:o_ + m],
                               lnT_hi[:, k, :], lnT_lo[:, k, :], k == 0, k == NT - 1)
                mm.then_inc(s[done], 1)

            def down(b, j, parts=range(IT)):
                if b == 0 and j == 0:
                    pe.wait_ge(s["split_lo"], 1 + IT)
                if parts[0]:
                    pass
                elif j >= 2:
                    pe.wait_ge(s["shared"], LT * b + j - 1)
                elif b < last_b:
                    pe.wait_ge(s["x1"], LT * (b + 1) + j + 3)
                else:
                    pe.wait_ge(s["place"], b + 1)
                tok = slice(j * P, (j + 1) * P)
                for c in parts:
                    pe.wait_ge(s["hlo"], IT * b + c + 1)
                    k = ORDER[c]
                    m = KI[k]
                    mm = three(bank[6 + j % 2][:, :], hT_hi[0:m, k, tok], hT_lo[0:m, k, tok],
                               sd_hi[0:m, k, :], sd_lo[0:m, k, :], c == 0, c == IT - 1)
                if parts[-1] == IT - 1:
                    mm.then_inc(s["dm"], 1)

            pe.wait_ge(s["w_in"], 16 * 2)
            project(0, 0)
            project(0, 1)
            for j in range(LT):
                energy(0, j)
            pe.wait_ge(s["const"], CONSTS)
            turn_prob(0, 0)
            project(1, 0)
            turn_prob(0, 1)
            project(1, 1)
            turn_prob(0, 2)
            turn_prob(0, 3)
            for b in range(NB):
                more = b < last_b
                mix(b)
                if b == 0:
                    energy(1, 0)
                    energy(1, 1)
                    energy(1, 2)
                    turn_ln2(0, 0)
                    turn_ln2(0, 1)
                    energy(1, 3)
                    turn_ln2(0, 2)
                    turn_ln2(0, 3)
                elif more:
                    project(b + 1, 0)
                    project(b + 1, 1)
                    down(b - 1, 0)
                    turn_ln2(b, 0)
                    turn_ln2(b, 1)
                    down(b - 1, 1)
                    turn_ln2(b, 2)
                    turn_ln2(b, 3)
                    down(b - 1, 2)
                    energy(b + 1, 0)
                    energy(b + 1, 1)
                    down(b - 1, 3)
                    energy(b + 1, 2)
                    energy(b + 1, 3)
                else:
                    down(b - 1, 0)
                    down(b - 1, 1)
                    turn_ln2(b, 0)
                    turn_ln2(b, 1)
                    down(b - 1, 2)
                    turn_ln2(b, 2)
                    turn_ln2(b, 3)
                    down(b - 1, 3)
                wide_shared(b, 0, 1)
                wide_shared(b, 0, 0)
                wide_shared(b, 1, 0)
                rank(b)
                wide_shared(b, 1, 1)
                if more:
                    turn_prob(b + 1, 0)
                    turn_prob(b + 1, 1)
                wide_shared(b, 2, 0)
                if more:
                    turn_prob(b + 1, 2)
                    turn_prob(b + 1, 3)
                wide_shared(b, 2, 1)
            for parts in (range(IT - 1), range(IT - 1, IT)):
                for j in range(2):
                    down(last_b, j, parts)
            for j in range(2, LT):
                down(last_b, j)

            def experts(q):
                w = pe.value_load(epack_i[0:1, bass.ds(q, 1)], min_val=0, max_val=E ** (2 * SLOTS - 1) - 1)
                return [(w // E ** i) % E for i in range(2 * SLOTS - 1)]

            def rows_in(u, r, q):
                pe.wait_ge(s_xl[r], 16 * (q + 1))
                at_least(pe, s["xev"], u)
                for k in range(NT):
                    mm = pe.transpose(bankXT[:, k * P:(k + 1) * P], xtb[:, r, k * P:(k + 1) * P], identb[:])
                mm.then_inc(s["cxt"], 1)

            def wide(u, v, e):
                pe.wait_ge(s["xev"], u + 1)
                at_least(pe, s["ch"], u - 1)
                for half_ in range(2):
                    for k in range(NT):
                        mm = pe.matmul(bank[2 * v + half_][:, 0:I], xTb[:, v, k, :], wgu(k, bass.ds(e, 1), half_ * I, I),
                                       start=(k == 0), stop=(k == NT - 1))
                mm.then_inc(s["cgu"], 1)

            def turn_hidden(u, v):
                pe.wait_ge(s["ch"], u + 1)
                at_least(pe, s["cev"], u)
                for k in range(IT):
                    mm = pe.transpose(bankHT[:, k * P:(k + 1) * P], hrow[:, v, k * P:(k + 1) * P], identb[:])
                mm.then_inc(s["ct"], 1)

            def narrow(u, v, e):
                if isinstance(u, int) and u == 0:
                    pe.wait_ge(s["shared"], TT)
                pe.wait_ge(s["cev"], u + 1)
                at_least(pe, s["yev"], u - 1)
                for k in range(IT):
                    mm = pe.matmul(bank[6 + v][:, :], hTb[0:KI[k], v, k, :], wd_sb[0:KI[k], k, bass.ds(e, 1), :],
                                   start=(k == 0), stop=(k == IT - 1))
                mm.then_inc(s["cy"], 1)

            def step(q, r, ids):
                u = SLOTS * q + r
                known = isinstance(u, int)
                if not known or 2 <= u <= NE + 1:
                    turn_hidden(u - 2, r % 2)
                if not known or u >= 3:
                    narrow(u - 3, (r - 3) % 2, ids[r])
                if not known or u + 1 < NE:
                    rows_in(u + 1, (r + 1) % SLOTS, q + 1 if r == SLOTS - 1 else q)
                if not known or u < NE:
                    wide(u, r % 2, ids[r + SLOTS - 1])

            pe.wait_ge(s["lnTlo"], TT)
            rows_in(0, 0, 0)
            pe.wait_ge(s["hid"], IT * NB)
            pe.wait_ge(s["packed"], 1)
            pe.wait_ge(s["wgu_in"], 16 * KP)
            pe.wait_ge(s["wgu2_in"], 16 * (NT - KP))
            pe.wait_ge(s["wd_in"], 16 * IT)
            for q in range(2):
                ids = experts(q)
                for r in range(SLOTS):
                    step(q, r, ids)
            with pe.Fori(2, QN) as q:
                ids = experts(q)
                for r in range(SLOTS):
                    step(q, r, ids)
            for u in range(SLOTS * QN, NE + 3):
                if u % SLOTS == 0:
                    ids = experts(u // SLOTS)
                step(u // SLOTS, u % SLOTS, ids)

            pe.wait_ge(s["yev"], NE)
            pe.wait_ge(s["za_in"], 16 * NB)
            for t in range(TT):
                pe.wait_ge(s_zl[t % ZS], 16 * (t // ZS + 1))
                at_least(pe, s["comb"], t - 3)
                pe.matmul(bank[t % 4][:, :], identb[:], za[:, t, :], start=True, stop=False)
                pe.matmul(bank[t % 4][:, :], identb[:], zb[:, t % ZS, :], start=False, stop=True).then_inc(s["zsum"], 1)

        @block.scalar
        def _(act):
            def leave(dst, n, done):
                act.copy(dst, bank[4 + n % 2][:, :].rearrange("p (k l) -> p k l", k=NT)).then_inc(s[done], 1)

            def qk(b):
                at_least(act, s["eng"], LT * b)
                for n, (dst, bias) in enumerate(((q_hi, bq_sb), (k_hi, bk_sb))):
                    act.wait_ge(s["proj"], 2 * b + n + 1)
                    act.activation(dst[:], bank[QK_BANK[b] + n][:, :], ACT.Identity, bias=bias[:]).then_inc(s["qhi"], 1)

            def x_high(b):
                act.wait_ge(s["xT_in"], 16 * (b + 1))
                at_least(act, s["xmm"], LT * b)
                act.copy(xT_hi[:], xT_raw[:]).then_inc(s["xThi"], 1)

            def soft(b, j):
                act.wait_ge(s["nmax"], LT * b + j + 1)
                at_least(act, s["tp"], LT * b)
                act.activation(prob[:, j, :], bank[j % 2][:, :], ACT.Exp, bias=nmx[:, j:j + 1],
                               accum_out=den[:, j:j + 1]).then_inc(s["expd"], 1)

            def normalise(b, j):
                act.wait_ge(s["rden"], LT * b + j + 1)
                act.activation(prob[:, j, :], prob[:, j, :], ACT.Identity, bias=less_mean[:],
                               scale=rden[:, j:j + 1]).then_inc(s["prb"], 1)

            def rows_again(b):
                act.wait_ge(s["ln2"], LT * (b + 1))
                at_least(act, s["scat"], 16 * TOP * LT * b)
                act.copy(lnb_rows[1], lnr2[:]).then_inc(s["rowsb2"], 1)

            def prob_high(b, j):
                at_least(act, s["xmm"], LT * b)
                act.wait_ge(s["tp"], LT * b + j + 1)
                leave(probT_hi[:, :, j * P:(j + 1) * P], j, "probT")

            def ln2_high(b, j):
                if b == 0:
                    act.wait_ge(s["split_lo"], 1)
                at_least(act, s["sup"], IT * b)
                act.wait_ge(s["t2"], LT * b + j + 1)
                leave(lnT_hi[:, :, j * P:(j + 1) * P], j, "lnThi")

            def gate_shared(b, c):
                n = IT * b + c
                m = KI[ORDER[c]]
                act.wait_ge(s["sgate"], n + 1)
                at_least(act, s["hlo"], n - 1)
                act.activation(sig[0:m, n % 2, :], bank[0 if c == 1 else 2][0:m, :], ACT.Sigmoid).then_inc(s["sigd"], 1)

            def hidden_high(b, c):
                n = IT * b + c
                m = KI[ORDER[c]]
                act.wait_ge(s["hid"], n + 1)
                at_least(act, s["dm"], LT * b)
                if n == 0:
                    act.wait_ge(s["split_lo"], 1 + IT)
                act.copy(hT_hi[0:m, ORDER[c], :], sig[0:m, n % 2, :]).then_inc(s["hhi"], 1)

            def logits_out(b):
                m = KI[IT - 1]
                act.wait_ge(s["sup"], IT * b + 1)
                at_least(act, s["lgT"], b)
                act.copy(lgT[:], bank[3][m:m + E, :]).then_inc(s["lgcopy"], 1)

            def add_ln2(b, j):
                act.wait_ge(s["coef"], b + 1)
                act.wait_ge(s["ln2"], LT * (b + 1))
                t = LT * b + j
                act.activation(acc[:, t, :], acc[:, t, :], ACT.Identity, bias=drop[:, j:j + 1],
                               scale=grow[:, j:j + 1]).then_inc(s["base"], 1)

            act.wait_ge(s["small_in"], 16 * 4)
            act.activation(tg[:, 0:2], g_sb[:], ACT.Tanh).then_inc(s["gates"], 1)
            act.activation(tg[:, 2:3], g_sb[:, 1:2], ACT.Tanh, scale=-1.0).then_inc(s["gates"], 1)
            qk(0)
            x_high(0)
            act.wait_ge(s["const"], CONSTS)
            soft(0, 0)
            soft(0, 1)
            normalise(0, 0)
            soft(0, 2)
            normalise(0, 1)
            soft(0, 3)
            normalise(0, 2)
            prob_high(0, 0)
            normalise(0, 3)
            for j in range(1, LT):
                prob_high(0, j)
            qk(1)
            act.wait_ge(s["sgu_in"], 16)
            act.copy(sgu_hi[:], sgu_raw[:]).then_inc(s["split_hi"], 1)
            act.wait_ge(s["sd_in"], 16 * IT)
            for k in range(IT):
                act.copy(sd_hi[0:KI[k], k, :], sd_raw[0:KI[k], k, :]).then_inc(s["split_hi"], 1)
            for b in range(NB):
                more = b < last_b
                if more:
                    x_high(b + 1)
                    if b:
                        qk(b + 1)
                    act.activation(warm[:], less_mean[:], ACT.Exp)
                if b == 0:
                    soft(1, 0)
                    soft(1, 1)
                ln2_high(b, 0)
                ln2_high(b, 1)
                if b == 0:
                    soft(1, 2)
                ln2_high(b, 2)
                ln2_high(b, 3)
                if b == 0:
                    soft(1, 3)
                rows_again(b)
                if 0 < b < last_b:
                    for j in range(LT):
                        soft(b + 1, j)
                logits_out(b)
                if more:
                    for j in range(LT):
                        normalise(b + 1, j)
                act.wait_ge(s["lgshift"], 2 * (b + 1))
                at_least(act, s["weight"], b)
                act.activation(rexp_sb[:], shifted[:], ACT.Exp).then_inc(s["rexp"], 1)
                gate_shared(b, 0)
                gate_shared(b, 1)
                add_ln2(b, 0)
                add_ln2(b, 1)
                hidden_high(b, 0)
                add_ln2(b, 2)
                add_ln2(b, 3)
                if more:
                    prob_high(b + 1, 0)
                    prob_high(b + 1, 1)
                hidden_high(b, 1)
                gate_shared(b, 2)
                if more:
                    prob_high(b + 1, 2)
                    prob_high(b + 1, 3)
                hidden_high(b, 2)

            def sigmoid(u, v):
                act.wait_ge(s["cgu"], u + 1)
                at_least(act, s["ch"], u - 1)
                act.activation(sigc[:, v, :], bank[2 * v][:, 0:I], ACT.Sigmoid).then_inc(s["csig"], 1)

            def hidden_out(u, v):
                act.wait_ge(s["ct"], u + 1)
                at_least(act, s["cy"], u - 1)
                act.copy(hTb[:, v], bankHT[:, 0:IT * P].rearrange("p (k l) -> p k l", k=IT)).then_inc(s["cev"], 1)

            def step(q, r):
                u = SLOTS * q + r
                known = isinstance(u, int)
                if not known or 1 <= u <= NE:
                    sigmoid(u - 1, (r - 1) % 2)
                if not known or 2 <= u <= NE + 1:
                    hidden_out(u - 2, r % 2)

            for r in range(SLOTS):
                step(0, r)
            with act.Fori(1, QN) as q:
                for r in range(SLOTS):
                    step(q, r)
            for u in range(SLOTS * QN, NE + 2):
                step(u // SLOTS, u % SLOTS)

        @block.vector
        def _(dve):
            V = nc.vector
            chain = [0]

            def link(ins):
                chain[0] += 1
                ins.then_inc(s["dchain"], 1)
                dve.wait_ge(s["dchain"], chain[0])

            def statistics(rows, n, b, j):
                link(V.bn_stats(out=st[n][:, j, :], in_=rows))
                V.bn_aggr(out=mv[n][:, j, :], in_=st[n][:, j, :]).then_inc(s[f"stat{n + 1}"], 1)

            def variance(n, b):
                dve.wait_ge(s[f"stat{n + 1}"], LT * (b + 1))
                V.tensor_scalar(ve[n][:], mv[n][:, :, 1], EPS, None, ALU.add).then_inc(s[f"var{n + 1}"], 1)

            def ln1_stats(b, j):
                dve.wait_ge(X_IN[b], 16)
                statistics(acc[:, LT * b + j, :], 0, b, j)

            def qk_low(b):
                for n, (dst, hi, bias) in enumerate(((q_lo, q_hi, bq_sb), (k_lo, k_hi, bk_sb))):
                    dve.wait_ge(s["qhi"], 2 * b + n + 1)
                    V.scalar_tensor_tensor(out=dst[:], in0=bank[QK_BANK[b] + n][:, :], scalar=bias[:], in1=hi[:].bitcast(F32),
                                           op0=ALU.add, op1=ALU.subtract).then_inc(s["qlo"], 1)

            def row_max(b, j):
                dve.wait_ge(s["eng"], LT * b + j + 1)
                V.tensor_reduce(nmx[:, j:j + 1], bank[j % 2][:, :], AX.X, ALU.max, negate=True).then_inc(s["nmax"], 1)

            def over_sum(b, j):
                dve.wait_ge(s["expd"], LT * b + j + 1)
                at_least(dve, s["prb"], LT * b)
                V.reciprocal(rden[:, j:j + 1], den[:, j:j + 1]).then_inc(s["rden"], 1)

            def residual(b):
                dve.wait_ge(s["rstd1"], b + 1)
                early = 0 < b < last_b
                if early:
                    ln1_stats(b + 1, 0)
                for j in range(LT):
                    t = LT * b + j
                    dve.wait_ge(s["xmm"], t + 1)
                    V.scalar_tensor_tensor(out=acc[:, t, :], in0=bank[6 + j % 2][:, :], scalar=rs[0][:, j:j + 1],
                                           in1=acc[:, t, :], op0=ALU.mult, op1=ALU.add).then_inc(s["x1"], 1)
                    dve.wait_ge(s["x1"], t + 1)
                    statistics(acc[:, t, :], 1, b, j)
                    if early and j + 1 < LT:
                        ln1_stats(b + 1, j + 1)

            def ln2_apply(b):
                variance(1, b)
                if 0 < b < last_b:
                    variance(0, b + 1)
                if b == 0:
                    row_max(1, 0)
                    row_max(1, 1)
                dve.wait_ge(s["rstd2"], b + 1)
                at_least(dve, s["t2"], LT * b)
                at_least(dve, s["rowsb"], b)
                at_least(dve, s["rowsb2"], b)
                for j in range(LT):
                    t = LT * b + j
                    V.tensor_scalar(lnr2[:, j, :], acc[:, t, :], mv[1][:, j, 0:1], rs[1][:, j:j + 1],
                                    ALU.subtract, ALU.mult).then_inc(s["ln2"], 1)

            def low(dst, hi, b, done_hi, done_lo, j):
                tok = slice(j * P, (j + 1) * P)
                dve.wait_ge(s[done_hi], LT * b + j + 1)
                V.tensor_tensor(dst[:, :, tok], bank[4 + j % 2][:, :].rearrange("p (k l) -> p k l", k=NT),
                                hi[:, :, tok].bitcast(F32), ALU.subtract).then_inc(s[done_lo], 1)

            def prob_low(b, j):
                at_least(dve, s["xmm"], LT * b)
                low(probT_lo, probT_hi, b, "probT", "probTlo", j)

            def ln2_low(b, j):
                at_least(dve, s["sup"], IT * b)
                if b == 0:
                    dve.wait_ge(s["split_lo"], 1)
                low(lnT_lo, lnT_hi, b, "lnThi", "lnTlo", j)

            def over_e(v):
                return v.rearrange("p (j a) -> p j a", a=1).to_broadcast([P, v.shape[1], E])

            def choose(b):
                lg = bank[7][:, 0:LT * E].rearrange("p (j e) -> p j e", e=E)
                dve.wait_ge(s["lgT"], b + 1)
                at_least(dve, s["order"], TOP * b)
                for c in range(TOP):
                    among = lg if c == 0 else ra[1][:]
                    link(V.tensor_reduce(rv[c][:], among, AX.X, ALU.max))
                    link(V.tensor_tensor(ra[2][:], among, over_e(rv[c][:]), ALU.is_equal))
                    link(V.tensor_tensor(ra[2][:], ra[2][:], down_idx[:], ALU.mult))
                    link(V.tensor_reduce(rank_of[:, c, :], ra[2][:], AX.X, ALU.max))
                    link(V.tensor_tensor(mask[c][:], down_idx[:], over_e(rank_of[:, c, :]), ALU.is_equal))
                    if c == 0:
                        link(V.scalar_tensor_tensor(out=ra[1][:], in0=mask[c][:], scalar=-TAKEN, in1=lg,
                                                    op0=ALU.mult, op1=ALU.add))
                V.tensor_tensor(picked[:], mask[0][:], mask[1][:], ALU.add).then_inc(s["pick"], 1)
                V.tensor_tensor(shifted[:, :, 0:E], lg, over_e(rv[0][:]), ALU.subtract).then_inc(s["lgshift"], 1)
                V.tensor_tensor(shifted[:, :, E], rv[1][:], rv[0][:], ALU.subtract).then_inc(s["lgshift"], 1)
                if b:
                    dve.wait_ge(s["scat"], 16 * TOP * LT * b)
                for c in range(TOP):
                    link(V.tensor_tensor(second[:, c, :], rank_of[:, c, :], rank_of[:, 1 - c, :], ALU.is_lt))
                    V.scalar_tensor_tensor(out=lnb[c][:, :, DST], in0=second[:, c, :], scalar=float(TOK),
                                           in1=token[:, LT * b:LT * (b + 1)], op0=ALU.mult, op1=ALU.add).then_inc(s["order"], 1)

            def weights(b):
                dve.wait_ge(s["rexp"], b + 1)
                link(V.tensor_reduce(rv[0][:], rexp_sb[:, :, 0:E], AX.X, ALU.add))
                link(V.reciprocal(rv[1][:], rv[0][:]))
                link(V.tensor_scalar(cwg[:, 0, :], rv[1][:], tg[:, 1:2], None, ALU.mult))
                V.tensor_tensor(cwg[:, 1, :], cwg[:, 0, :], rexp_sb[:, :, E], ALU.mult).then_inc(s["weight"], 1)

            def places(b):
                dve.wait_ge(s["rank"], b + 1)
                totals = bank[6][:, LT * E:2 * LT * E].rearrange("p (j e) -> p e j", e=E)
                link(V.tensor_copy(tot[:], totals))
                flat = lambda v: v[:].rearrange("p e j -> p (e j)")
                link(V.tensor_tensor_scan(flat(upto), flat(reset), flat(tot), 0.0, ALU.mult, ALU.add))
                link(V.tensor_tensor(before[:], upto[:], tot[:], ALU.subtract))
                link(V.tensor_tensor(before[:], before[:],
                                     filled[:, 0:E].rearrange("p (e a) -> p e a", a=1).to_broadcast([P, E, LT]), ALU.add))
                link(V.tensor_tensor(filled[:, 0:E], filled[:, 0:E], upto[:, :, LT - 1], ALU.add))
                V.tensor_tensor(ra[0][:], bank[6][:, 0:LT * E].rearrange("p (j e) -> p j e", e=E),
                                before[:].rearrange("p e j -> p j e"), ALU.add).then_inc(s["place"], 1)
                dve.wait_ge(s["place"], b + 1)
                for c in range(TOP):
                    link(V.tensor_tensor(ra[2][:], mask[c][:], ra[0][:], ALU.mult))
                    link(V.tensor_reduce(rv[c][:], ra[2][:], AX.X, ALU.add))
                at_least(dve, s["scat"], 16 * TOP * LT * b)
                link(V.tensor_copy(slot[:, 0, :], rv[0][:]))
                V.tensor_copy(slot[:, 1, :], rv[1][:]).then_inc(s["placed"], 1)

            across = lambda v: v[:].rearrange("p (a e) -> p a e", a=1).to_broadcast([P, NE, E])
            start = big[:, 0:NE]

            def tables_tiles():
                link(V.tensor_tensor(cnt[:], filled[:, 0:E], region0[:], ALU.subtract))
                link(V.tensor_tensor(ahead[:], filled[:, 1:E + 1], filled[:, 0:E], ALU.subtract))
                parts = big[:].rearrange("p t e -> p (t e)")[:, 0:E * TT].rearrange("p (e j) -> p e j", e=E)
                link(V.tensor_tensor(parts, cnt[:].rearrange("p (e a) -> p e a", a=1).to_broadcast([P, E, TT]),
                                     fill_at[:].rearrange("p (a j) -> p a j", a=1).to_broadcast([P, E, TT]), ALU.is_gt))
                link(V.tensor_reduce(ntile[:], parts, AX.X, ALU.add))
                link(V.tensor_tensor_scan(tend[:], ones[:, 0:E], ntile[:], 0.0, ALU.mult, ALU.add))
                link(V.tensor_scalar(skip[:], ntile[:], -float(P), float(REG), ALU.mult, ALU.add))
                link(V.tensor_tensor(start, over_e(tile_no[:, 0:NE]), across(tend), ALU.is_ge))

            def tables_limits():
                link(V.tensor_tensor(big2[:], start, across(ahead), ALU.mult))
                link(V.tensor_reduce(limit[:], big2[:], AX.X, ALU.add))
                link(V.tensor_scalar(limit[:], limit[:], filled[:, 0:1], -float(P), ALU.add, ALU.add))

            def tables_rows():
                link(V.tensor_tensor(big2[:], start, across(skip), ALU.mult))
                link(V.tensor_reduce(tf[:], big2[:], AX.X, ALU.add))
                link(V.tensor_tensor(tf[:], tf[:], tile_row[:], ALU.add))
                V.tensor_tensor(erow[:], tf[:], limit[:], ALU.min).then_inc(s["tabs"], 1)

            def tables_again():
                link(V.tensor_tensor(over[:], tf[:], limit[:], ALU.subtract))
                link(V.scalar_tensor_tensor(out=again[:], in0=over[:], scalar=part[:], in1=unused_at[:],
                                            op0=ALU.is_gt, op1=ALU.mult))

            def tables_experts():
                link(V.tensor_reduce(tf[:], start, AX.X, ALU.add))
                link(V.tensor_scalar(etab[:, SLOTS:SLOTS + NE], tf[:], float(E - 1), None, ALU.min))
                steps = etab[:].rearrange("p (q r) -> p q r", r=SLOTS)
                mine = powers[:].rearrange("p (a i) -> p a i", a=1)
                V.tensor_tensor(digits[:, :, 0:SLOTS - 1], steps[:, 0:NQ, 1:SLOTS],
                                mine[:, :, 0:SLOTS - 1].to_broadcast([P, NQ, SLOTS - 1]), ALU.mult)
                link(V.tensor_tensor(digits[:, :, SLOTS - 1:], steps[:, 1:NQ + 1, :],
                                     mine[:, :, SLOTS - 1:].to_broadcast([P, NQ, SLOTS]), ALU.mult))
                link(V.tensor_reduce(epack[:], digits[:], AX.X, ALU.add))
                V.tensor_copy(epack_i[:], epack[:]).then_inc(s["packed"], 1)

            def tables_sent():
                link(V.tensor_scalar(slot_rows[:], tile_no[:].rearrange("p (q r) -> p r q", r=SLOTS), tend[:, E - 2:E - 1], None, ALU.is_lt))
                link(V.tensor_reduce(slot_sum[:], slot_rows[:], AX.X, ALU.add))
                V.tensor_scalar(sent_i[:], slot_sum[:], 1.0, 16.0, ALU.max, ALU.mult).then_inc(s["sent"], 1)

            def shared_hidden(b, c):
                n = IT * b + c
                m = KI[ORDER[c]]
                dve.wait_ge(s["sigd"], n + 1)
                dve.wait_ge(s["sup"], n + 1)
                V.tensor_tensor(sig[0:m, n % 2, :], sig[0:m, n % 2, :], bank[1 if c == 1 else 3][0:m, :], ALU.mult).then_inc(s["hid"], 1)

            def hidden_low_last(c):
                n = IT * last_b + c
                k = ORDER[c]
                m = KI[k]
                dve.wait_ge(s["hhi"], n + 1)
                dve.wait_ge(s["hlo"], n)
                V.tensor_tensor(hT_lo[0:m, k, :], sig[0:m, n % 2, :], hT_hi[0:m, k, :].bitcast(F32),
                                ALU.subtract).then_inc(s["hlo"], 1)

            def shared_out(b, j):
                t = LT * b + j
                dve.wait_ge(s["dm"], t + 1)
                dve.wait_ge(s["base"], t + 1)
                V.scalar_tensor_tensor(out=acc[:, t, :], in0=bank[6 + j % 2][:, :], scalar=tg[:, 1:2],
                                       in1=acc[:, t, :], op0=ALU.mult, op1=ALU.add).then_inc(s["shared"], 1)

            dve.wait_ge(s["small_in"], 16 * 4)
            qk_low(0)
            ln1_stats(0, 0)
            row_max(0, 0)
            row_max(0, 1)
            over_sum(0, 0)
            row_max(0, 2)
            over_sum(0, 1)
            row_max(0, 3)
            over_sum(0, 2)
            over_sum(0, 3)
            dve.wait_ge(s["const"], CONSTS)
            dve.wait_ge(s["gates"], 2)
            prob_low(0, 0)
            prob_low(0, 1)
            ln1_stats(0, 1)
            prob_low(0, 2)
            prob_low(0, 3)
            ln1_stats(0, 2)
            ln1_stats(0, 3)
            variance(0, 0)
            for b in range(NB):
                more = b < last_b
                if b == 0:
                    qk_low(1)
                residual(b)
                ln2_apply(b)
                if 0 < b < last_b:
                    qk_low(b + 1)
                if b == 0:
                    row_max(1, 2)
                    ln2_low(0, 0)
                    ln2_low(0, 1)
                    ln2_low(0, 2)
                    ln2_low(0, 3)
                    row_max(1, 3)
                else:
                    if more:
                        ln2_low(b, 0)
                        shared_out(b - 1, 0)
                    else:
                        shared_out(b - 1, 0)
                        ln2_low(b, 0)
                    ln2_low(b, 1)
                    shared_out(b - 1, 1)
                    ln2_low(b, 2)
                    ln2_low(b, 3)
                    shared_out(b - 1, 2)
                    if more:
                        row_max(b + 1, 0)
                        row_max(b + 1, 1)
                    shared_out(b - 1, 3)
                if 0 < b < last_b:
                    row_max(b + 1, 2)
                    row_max(b + 1, 3)
                if more:
                    for j in range(LT):
                        over_sum(b + 1, j)
                if b == 0:
                    for j in range(LT):
                        ln1_stats(1, j)
                    variance(0, 1)
                choose(b)
                weights(b)
                places(b)
                shared_hidden(b, 0)
                shared_hidden(b, 1)
                if more:
                    for j in range(LT):
                        prob_low(b + 1, j)
                else:
                    hidden_low_last(0)
                    tables_tiles()
                    hidden_low_last(1)
                    tables_limits()
                shared_hidden(b, 2)
            hidden_low_last(2)
            link(V.memset(hrow[:, :, I:IT * P], 0.0))
            tables_rows()
            shared_out(last_b, 0)
            shared_out(last_b, 1)
            tables_again()
            tables_experts()
            shared_out(last_b, 2)
            tables_sent()

            def rows_out(u, r):
                dve.wait_ge(s["cxt"], u + 1)
                at_least(dve, s["cgu"], u - 1)
                V.tensor_tensor(dest[:, bass.ds(u, 1)], xt[:, r, DST:DST + 1], again[:, bass.ds(u, 1)], ALU.max)
                V.tensor_copy(wt[:, bass.ds(u, 1)], xt[:, r, WT:WT + 1])
                V.tensor_copy(xTb[:, r % 2], bankXT[:, 0:N].rearrange("p (k l) -> p k l", k=NT)).then_inc(s["xev"], 1)

            def hidden(u, v):
                dve.wait_ge(s["csig"], u + 1)
                at_least(dve, s["ct"], u - 1)
                V.tensor_tensor(hrow[:, v, 0:I], sigc[:, v, :], bank[2 * v + 1][:, 0:I], ALU.mult).then_inc(s["ch"], 1)

            def result(u, v, slot_, q):
                dve.wait_ge(s["cy"], u + 1)
                if not isinstance(q, int) or q > 0:
                    dve.wait_ge(s_yd[slot_], 16 * q)
                V.tensor_scalar(ysb[:, slot_, :], bank[6 + v][:, :], wt[:, bass.ds(u, 1)].bitcast(F32), None,
                                ALU.mult).then_inc(s["yev"], 1)

            def step(q, r):
                u = SLOTS * q + r
                known = isinstance(u, int)
                if not known or 1 <= u <= NE:
                    hidden(u - 1, (r - 1) % 2)
                if not known or 3 <= u:
                    result(u - 3, (r - 3) % 2, (r - 3) % SLOTS, q if r == 3 else q - 1)
                if not known or u + 1 < NE:
                    rows_out(u + 1, (r + 1) % SLOTS)

            rows_out(0, 0)
            shared_out(last_b, 3)
            for q in range(2):
                for r in range(SLOTS):
                    step(q, r)
            with dve.Fori(2, QN) as q:
                for r in range(SLOTS):
                    step(q, r)
            for u in range(SLOTS * QN, NE + 3):
                step(u // SLOTS, u % SLOTS)

            for t in range(TT):
                dve.wait_ge(s["zsum"], t + 1)
                V.tensor_tensor(acc[:, t, :], bank[t % 4][:, :], acc[:, t, :], ALU.add).then_inc(s["comb"], 1)


def kernel(x, ctx_1024, g_xattn, g_ffn, L0_xattn_Wq, L0_xattn_bq, L0_xattn_Wk, L0_xattn_bk, L0_ffn_router_w,
           L0_ffn_shared_gate, L0_ffn_shared_up, L0_ffn_shared_down, L0_ffn_w_gate, L0_ffn_w_up, L0_ffn_w_down):
    import numpy as np
    import concourse.bacc as bacc
    from concourse import mybir as mb
    from concourse.bass_utils import run_bass_kernel_spmd

    T = lambda a: np.asarray(a).swapaxes(-1, -2)
    arrays = {
        "x": x, "xT": T(x), "ctxT": T(ctx_1024), "g2": np.stack([np.asarray(g_xattn), np.asarray(g_ffn)]),
        "wqT": T(L0_xattn_Wq), "wkT": T(L0_xattn_Wk), "bq": L0_xattn_bq, "bk": L0_xattn_bk,
        "sguT": np.concatenate([T(L0_ffn_shared_gate), T(L0_ffn_shared_up), T(L0_ffn_router_w)], 1),
        "sdT": T(L0_ffn_shared_down),
        "wguT": np.concatenate([T(L0_ffn_w_gate), T(L0_ffn_w_up)], 2), "wdT": T(L0_ffn_w_down),
    }
    arrays = {n: np.ascontiguousarray(a) for n, a in arrays.items()}
    nc = bacc.Bacc("TRN2", target_bir_lowering=False, num_devices=1)
    args = [nc.dram_tensor(n, a.shape, mb.dt.from_np(a.dtype), kind="ExternalInput").ap() for n, a in arrays.items()]
    shape = np.asarray(x).shape
    o = nc.dram_tensor("out", (shape[0] * shape[1], shape[2]), mb.dt.float32, kind="ExternalOutput").ap()
    gated_block(nc, *args, o)
    r = run_bass_kernel_spmd(nc, [arrays], core_ids=[0])
    return np.asarray(r.results[0]["out"]).reshape(shape)
```
